# Optimizing a Trainium2 kernel written in Bass

```python
import numpy as np
import jax
import jax.numpy as jnp

def _softmax(x, axis=-1):
    return jax.nn.softmax(x, axis=axis)

def _gelu(x):
    return jax.nn.gelu(x, approximate=True)

def _silu(x):
    return jax.nn.silu(x)

def _sigmoid(x):
    return jax.nn.sigmoid(x)

def _layernorm(x, axis=-1, eps=1e-05):
    m = jnp.mean(x, axis=axis, keepdims=True)
    v = jnp.var(x, axis=axis, keepdims=True)
    return (x - m) / jnp.sqrt(v + eps)

def _scatter_add(tgt, idx, src, axis=0):
    return tgt.at[idx].add(src)

def _segment_sum(src, seg, n):
    return jax.ops.segment_sum(src, seg, n)
kernel_name = 'mk_recurrent_d2_jaxref_r8_7cdef3'

def setup_inputs(seed: int=0):
    np.random.seed(seed)
    _w = jnp.asarray

    def _L0_attn_setup():
        import jax, jax.numpy as jnp
        import numpy as np
        HIDDEN = 128
        TILE = 128
        key = jax.random.key(seed)
        ks = jax.random.split(key, 9)
        B, S, D = (2, 512, HIDDEN)
        s = 1.0 / np.sqrt(D)
        return {'batch': jax.random.normal(ks[0], (B, S, D), jnp.float32), 'Wq': jax.random.normal(ks[1], (D, D), jnp.float32) * s, 'bq': jax.random.normal(ks[2], (D,), jnp.float32) * 0.01, 'Wk': jax.random.normal(ks[3], (D, D), jnp.float32) * s, 'bk': jax.random.normal(ks[4], (D,), jnp.float32) * 0.01, 'Wv': jax.random.normal(ks[5], (D, D), jnp.float32) * s, 'bv': jax.random.normal(ks[6], (D,), jnp.float32) * 0.01, 'Wo': jax.random.normal(ks[7], (D, D), jnp.float32) * s, 'bo': jax.random.normal(ks[8], (D,), jnp.float32) * 0.01}
    _L0_attn_in = _L0_attn_setup()

    def _L0_ffn_setup():
        import jax, jax.numpy as jnp
        import numpy as np
        EPS = 1e-05

        def _layernorm(x, w, b):
            mu = jnp.mean(x, axis=-1, keepdims=True)
            var = jnp.mean((x - mu) ** 2, axis=-1, keepdims=True)
            return (x - mu) * jax.lax.rsqrt(var + EPS) * w + b

        def _rope_tables(T, D, base=10000.0):
            inv_freq = 1.0 / base ** (jnp.arange(0, D, 2, dtype=jnp.float32) / D)
            t = jnp.arange(T, dtype=jnp.float32)
            freqs = jnp.einsum('i,j->ij', t, inv_freq)
            emb = jnp.concatenate([freqs, freqs], axis=-1)
            return (jnp.cos(emb), jnp.sin(emb))

        def _rotate_half(x):
            x1, x2 = (x[..., :x.shape[-1] // 2], x[..., x.shape[-1] // 2:])
            return jnp.concatenate([-x2, x1], axis=-1)

        def _attn(x, ln_w, ln_b, conv_w, attn_w, proj_w, n_head):
            B, T, C = x.shape
            D = C // n_head
            h = _layernorm(x, ln_w, ln_b)
            hc = jnp.transpose(h, (0, 2, 1))
            hc = jnp.pad(hc, ((0, 0), (0, 0), (2, 0)))
            hc = jax.lax.conv_general_dilated(hc, conv_w, window_strides=(1,), padding='VALID', dimension_numbers=('NCH', 'OIH', 'NCH'), feature_group_count=C)
            h = jnp.transpose(hc, (0, 2, 1))
            qkv = h @ attn_w
            q, k, v = jnp.split(qkv, 3, axis=-1)
            q = q.reshape(B, T, n_head, D)
            k = k.reshape(B, T, n_head, D)
            v = v.reshape(B, T, n_head, D)
            cos, sin = _rope_tables(T, D)
            cos = cos[None, :, None, :]
            sin = sin[None, :, None, :]
            q = q * cos + _rotate_half(q) * sin
            k = k * cos + _rotate_half(k) * sin
            scores = jnp.einsum('bqhd,bkhd->bhqk', q, k) / jnp.sqrt(jnp.float32(D))
            causal = jnp.tril(jnp.ones((T, T), dtype=bool))
            scores = jnp.where(causal, scores, jnp.float32(-1e+30))
            p = jax.nn.softmax(scores, axis=-1)
            y = jnp.einsum('bhqk,bkhd->bqhd', p, v).reshape(B, T, C)
            return y @ proj_w

        def _moe(x, ln_w, ln_b, router_w, expert_wv, expert_proj):
            h = _layernorm(x, ln_w, ln_b)
            logits = h @ router_w
            expert_idx = jnp.argmax(logits, axis=-1)
            E = router_w.shape[-1]
            out = jnp.zeros_like(x)
            for e in range(E):
                gv = h @ expert_wv[e]
                gate_raw, value = jnp.split(gv, 2, axis=-1)
                y = gate_raw * jax.nn.sigmoid(gate_raw) * value @ expert_proj[e]
                out = out + jnp.where((expert_idx == e)[..., None], y, 0.0)
            return out
        C, H, E, B, T = (128, 16, 4, 4, 128)
        Dff = 4 * C
        key = jax.random.key(seed)
        ks = jax.random.split(key, 8)
        s = 0.02
        return {'x': jax.random.normal(ks[0], (B, T, C), dtype=jnp.float32), 'ln1_w': jnp.ones((C,), jnp.float32), 'ln1_b': jnp.zeros((C,), jnp.float32), 'ln2_w': jnp.ones((C,), jnp.float32), 'ln2_b': jnp.zeros((C,), jnp.float32), 'conv_w': jax.random.normal(ks[1], (C, 1, 3), dtype=jnp.float32) * 0.1, 'attn_w': jax.random.normal(ks[2], (C, 3 * C), dtype=jnp.float32) * s, 'proj_w': jax.random.normal(ks[3], (C, C), dtype=jnp.float32) * s, 'router_w': jax.random.normal(ks[4], (C, E), dtype=jnp.float32) * s, 'expert_wv': jax.random.normal(ks[5], (E, C, 2 * Dff), dtype=jnp.float32) * s, 'expert_proj': jax.random.normal(ks[6], (E, Dff, C), dtype=jnp.float32) * s}
    _L0_ffn_in = _L0_ffn_setup()

    def _L1_attn_setup():
        import jax, jax.numpy as jnp
        import numpy as np
        D = 128
        H = 16
        DH = D // H
        key = jax.random.key(seed)
        k1, k2, k3 = jax.random.split(key, 3)
        x = jax.random.normal(k1, (2, 256, D), dtype=jnp.float32)
        w_qkv = jax.random.normal(k2, (3 * D, D), dtype=jnp.float32) * D ** (-0.5)
        w_proj = jax.random.normal(k3, (D, D), dtype=jnp.float32) * D ** (-0.5)
        return {'x': x, 'w_qkv': w_qkv, 'w_proj': w_proj}
    _L1_attn_in = _L1_attn_setup()

    def _L1_ffn_setup():
        import jax, jax.numpy as jnp
        import numpy as np
        DIM = 128
        DEPTH = 6
        HEADS = 16
        DIM_HEAD = 64
        WINDOW = 32
        INNER = HEADS * DIM_HEAD
        DIM_INNER = int(DIM * 4 * 2 / 3)
        QK_SCALE = 8.0

        def shift_tokens(t):
            a, s = jnp.split(t, 2, -1)
            s = jnp.pad(s, ((0, 0), (1, 0), (0, 0)))[:, :-1]
            return jnp.concatenate([a, s], -1)

        def l2norm(t):
            return t / jnp.maximum(jnp.linalg.norm(t, axis=-1, keepdims=True), 1e-12)

        def rotate_half(x):
            x1, x2 = jnp.split(x, 2, -1)
            return jnp.concatenate([-x2, x1], -1)

        def rotary_tables(n):
            half = jnp.arange(0, DIM_HEAD, 2, dtype=jnp.float32)
            inv_freq = 1.0 / 10000.0 ** (half / DIM_HEAD)
            t = jnp.arange(n, dtype=jnp.float32)
            freqs = t[:, None] * inv_freq[None, :]
            freqs = jnp.concatenate([freqs, freqs], -1)
            base_scale = (half + 0.4 * DIM_HEAD) / (1.4 * DIM_HEAD)
            power = (t - n // 2) / (WINDOW // 2)
            scale = base_scale[None, :] ** power[:, None]
            scale = jnp.concatenate([scale, scale], -1)
            return (freqs, scale)

        def local_attention(q, k, v):
            b, h, n, d = q.shape
            w = WINDOW
            nw = n // w
            bq = q.reshape(b, h, nw, w, d)
            bk = k.reshape(b, h, nw, w, d)
            bv = v.reshape(b, h, nw, w, d)

            def look(t):
                p = jnp.pad(t, ((0, 0), (0, 0), (1, 0), (0, 0), (0, 0)))
                return jnp.concatenate([p[:, :, :nw], p[:, :, 1:]], axis=3)
            bk2, bv2 = (look(bk), look(bv))
            seq = jnp.arange(n).reshape(nw, w)
            seq_p = jnp.pad(seq, ((1, 0), (0, 0)), constant_values=-1)
            jt = jnp.concatenate([seq_p[:nw], seq_p[1:]], axis=1)
            it = seq[:, :, None]
            jb = jt[:, None, :]
            mask = (it < jb) | (it > jb + w) | (jb == -1)
            sim = jnp.einsum('bhwie,bhwje->bhwij', bq, bk2) * QK_SCALE
            sim = jnp.where(mask, -jnp.finfo(sim.dtype).max, sim)
            attn = jax.nn.softmax(sim, -1)
            out = jnp.einsum('bhwij,bhwje->bhwie', attn, bv2)
            return out.reshape(b, h, n, d)

        def attn_layer(x, Wqkv, qs, ksc, Wo):
            b, n, _ = x.shape
            qkv = x @ Wqkv
            q, k, v = jnp.split(qkv, 3, -1)
            sh = lambda t: t.reshape(b, n, HEADS, DIM_HEAD).transpose(0, 2, 1, 3)
            q, k, v = (sh(q), sh(k), sh(v))
            q = l2norm(q) * qs
            k = l2norm(k) * ksc
            freqs, scale = rotary_tables(n)
            cos, sin = (jnp.cos(freqs), jnp.sin(freqs))
            q = q * cos * scale + rotate_half(q) * sin * scale
            inv = 1.0 / scale
            k = k * cos * inv + rotate_half(k) * sin * inv
            out = local_attention(q, k, v)
            out = out.transpose(0, 2, 1, 3).reshape(b, n, INNER)
            return out @ Wo

        def ffn_layer(x, g, bln, W1, b1, W2, b2):
            mu = x.mean(-1, keepdims=True)
            var = ((x - mu) ** 2).mean(-1, keepdims=True)
            xn = (x - mu) / jnp.sqrt(var + 1e-05) * g + bln
            hg = xn @ W1 + b1
            a, gate = jnp.split(hg, 2, -1)
            return a * jax.nn.gelu(gate, approximate=False) @ W2 + b2
        key = jax.random.key(seed)
        ks = jax.random.split(key, 8)
        B, N = (2, 256)
        init = lambda k, shape: jax.random.normal(k, shape, jnp.float32) * 0.02
        return {'x': jax.random.normal(ks[0], (B, N, DIM), jnp.float32), 'Wqkv': init(ks[1], (DEPTH, DIM, 3 * INNER)), 'q_scale': jnp.ones((DEPTH, DIM_HEAD), jnp.float32), 'k_scale': jnp.ones((DEPTH, DIM_HEAD), jnp.float32), 'Wo': init(ks[2], (DEPTH, INNER, DIM)), 'ln_g': jnp.ones((DEPTH, DIM), jnp.float32), 'ln_b': jnp.zeros((DEPTH, DIM), jnp.float32), 'W1': init(ks[3], (DEPTH, DIM, 2 * DIM_INNER)), 'b1': jnp.zeros((DEPTH, 2 * DIM_INNER), jnp.float32), 'W2': init(ks[4], (DEPTH, DIM_INNER, DIM)), 'b2': jnp.zeros((DEPTH, DIM), jnp.float32)}
    _L1_ffn_in = _L1_ffn_setup()
    _d = {'L0_attn_batch': _L0_attn_in['batch'], 'L0_attn_Wq': _L0_attn_in['Wq'], 'L0_attn_bq': _L0_attn_in['bq'], 'L0_attn_Wk': _L0_attn_in['Wk'], 'L0_attn_bk': _L0_attn_in['bk'], 'L0_attn_Wv': _L0_attn_in['Wv'], 'L0_attn_bv': _L0_attn_in['bv'], 'L0_attn_Wo': _L0_attn_in['Wo'], 'L0_attn_bo': _L0_attn_in['bo'], 'L0_ffn_ln1_w': _L0_ffn_in['ln1_w'], 'L0_ffn_ln1_b': _L0_ffn_in['ln1_b'], 'L0_ffn_ln2_w': _L0_ffn_in['ln2_w'], 'L0_ffn_ln2_b': _L0_ffn_in['ln2_b'], 'L0_ffn_conv_w': _L0_ffn_in['conv_w'], 'L0_ffn_attn_w': _L0_ffn_in['attn_w'], 'L0_ffn_proj_w': _L0_ffn_in['proj_w'], 'L0_ffn_router_w': _L0_ffn_in['router_w'], 'L0_ffn_expert_wv': _L0_ffn_in['expert_wv'], 'L0_ffn_expert_proj': _L0_ffn_in['expert_proj'], 'L1_attn_w_qkv': _L1_attn_in['w_qkv'], 'L1_attn_w_proj': _L1_attn_in['w_proj'], 'L1_ffn_Wqkv': _L1_ffn_in['Wqkv'], 'L1_ffn_q_scale': _L1_ffn_in['q_scale'], 'L1_ffn_k_scale': _L1_ffn_in['k_scale'], 'L1_ffn_Wo': _L1_ffn_in['Wo'], 'L1_ffn_ln_g': _L1_ffn_in['ln_g'], 'L1_ffn_ln_b': _L1_ffn_in['ln_b'], 'L1_ffn_W1': _L1_ffn_in['W1'], 'L1_ffn_b1': _L1_ffn_in['b1'], 'L1_ffn_W2': _L1_ffn_in['W2'], 'L1_ffn_b2': _L1_ffn_in['b2']}
    _x0 = _d['L0_attn_batch']
    _d['L0_attn_batch'] = jax.random.normal(jax.random.fold_in(jax.random.key(seed), 1), (4, 1024, 128), dtype=_x0.dtype)
    del _x0
    return _d

def reference(L0_attn_batch, L0_attn_Wq, L0_attn_bq, L0_attn_Wk, L0_attn_bk, L0_attn_Wv, L0_attn_bv, L0_attn_Wo, L0_attn_bo, L0_ffn_ln1_w, L0_ffn_ln1_b, L0_ffn_ln2_w, L0_ffn_ln2_b, L0_ffn_conv_w, L0_ffn_attn_w, L0_ffn_proj_w, L0_ffn_router_w, L0_ffn_expert_wv, L0_ffn_expert_proj, L1_attn_w_qkv, L1_attn_w_proj, L1_ffn_Wqkv, L1_ffn_q_scale, L1_ffn_k_scale, L1_ffn_Wo, L1_ffn_ln_g, L1_ffn_ln_b, L1_ffn_W1, L1_ffn_b1, L1_ffn_W2, L1_ffn_b2):

    def _L0_attn_ref(batch, Wq, bq, Wk, bk, Wv, bv, Wo, bo):
        import jax, jax.numpy as jnp
        import numpy as np
        HIDDEN = 128
        TILE = 128
        B, S, D = batch.shape
        scale = 1.0 / np.sqrt(D)
        T = S // TILE
        q = batch @ Wq.T + bq
        k = batch @ Wk.T + bk
        v = batch @ Wv.T + bv
        k_t = k.reshape(B, T, TILE, D)
        v_t = v.reshape(B, T, TILE, D)
        scores = jnp.einsum('bqd,btkd->btqk', q, k_t) * scale
        w = jax.nn.softmax(scores, axis=-1)
        out = jnp.einsum('btqk,btkd->bqd', w, v_t)
        norm = w.sum(axis=-1).sum(axis=1)[..., None]
        out = out / (norm + 1e-06)
        return out @ Wo.T + bo

    def _L0_ffn_ref(x, ln1_w, ln1_b, ln2_w, ln2_b, conv_w, attn_w, proj_w, router_w, expert_wv, expert_proj):
        import jax, jax.numpy as jnp
        import numpy as np
        EPS = 1e-05

        def _layernorm(x, w, b):
            mu = jnp.mean(x, axis=-1, keepdims=True)
            var = jnp.mean((x - mu) ** 2, axis=-1, keepdims=True)
            return (x - mu) * jax.lax.rsqrt(var + EPS) * w + b

        def _rope_tables(T, D, base=10000.0):
            inv_freq = 1.0 / base ** (jnp.arange(0, D, 2, dtype=jnp.float32) / D)
            t = jnp.arange(T, dtype=jnp.float32)
            freqs = jnp.einsum('i,j->ij', t, inv_freq)
            emb = jnp.concatenate([freqs, freqs], axis=-1)
            return (jnp.cos(emb), jnp.sin(emb))

        def _rotate_half(x):
            x1, x2 = (x[..., :x.shape[-1] // 2], x[..., x.shape[-1] // 2:])
            return jnp.concatenate([-x2, x1], axis=-1)

        def _attn(x, ln_w, ln_b, conv_w, attn_w, proj_w, n_head):
            B, T, C = x.shape
            D = C // n_head
            h = _layernorm(x, ln_w, ln_b)
            hc = jnp.transpose(h, (0, 2, 1))
            hc = jnp.pad(hc, ((0, 0), (0, 0), (2, 0)))
            hc = jax.lax.conv_general_dilated(hc, conv_w, window_strides=(1,), padding='VALID', dimension_numbers=('NCH', 'OIH', 'NCH'), feature_group_count=C)
            h = jnp.transpose(hc, (0, 2, 1))
            qkv = h @ attn_w
            q, k, v = jnp.split(qkv, 3, axis=-1)
            q = q.reshape(B, T, n_head, D)
            k = k.reshape(B, T, n_head, D)
            v = v.reshape(B, T, n_head, D)
            cos, sin = _rope_tables(T, D)
            cos = cos[None, :, None, :]
            sin = sin[None, :, None, :]
            q = q * cos + _rotate_half(q) * sin
            k = k * cos + _rotate_half(k) * sin
            scores = jnp.einsum('bqhd,bkhd->bhqk', q, k) / jnp.sqrt(jnp.float32(D))
            causal = jnp.tril(jnp.ones((T, T), dtype=bool))
            scores = jnp.where(causal, scores, jnp.float32(-1e+30))
            p = jax.nn.softmax(scores, axis=-1)
            y = jnp.einsum('bhqk,bkhd->bqhd', p, v).reshape(B, T, C)
            return y @ proj_w

        def _moe(x, ln_w, ln_b, router_w, expert_wv, expert_proj):
            h = _layernorm(x, ln_w, ln_b)
            logits = h @ router_w
            expert_idx = jnp.argmax(logits, axis=-1)
            E = router_w.shape[-1]
            out = jnp.zeros_like(x)
            for e in range(E):
                gv = h @ expert_wv[e]
                gate_raw, value = jnp.split(gv, 2, axis=-1)
                y = gate_raw * jax.nn.sigmoid(gate_raw) * value @ expert_proj[e]
                out = out + jnp.where((expert_idx == e)[..., None], y, 0.0)
            return out
        n_head = 16
        x = x + _attn(x, ln1_w, ln1_b, conv_w, attn_w, proj_w, n_head)
        x = x + _moe(x, ln2_w, ln2_b, router_w, expert_wv, expert_proj)
        return x

    def _L1_attn_ref(x, w_qkv, w_proj):
        import jax, jax.numpy as jnp
        import numpy as np
        D = 128
        H = 16
        DH = D // H
        B, L, _ = x.shape
        qkv = x @ w_qkv.T
        q, k, v = jnp.split(qkv, 3, axis=-1)
        q = q.reshape(B, L, H, DH)
        k = k.reshape(B, L, H, DH)
        v = v.reshape(B, L, H, DH)
        scale = 1.0 / np.sqrt(DH)
        scores = jnp.einsum('blhd,bmhd->bhlm', q, k) * scale
        causal = jnp.arange(L)[:, None] < jnp.arange(L)[None, :]
        scores = jnp.where(causal[None, None, :, :], -jnp.inf, scores)
        att = jax.nn.softmax(scores, axis=-1)
        out = jnp.einsum('bhlm,bmhd->blhd', att, v)
        out = out.reshape(B, L, D)
        return out @ w_proj.T

    def _L1_ffn_ref(x, Wqkv, q_scale, k_scale, Wo, ln_g, ln_b, W1, b1, W2, b2):
        import jax, jax.numpy as jnp
        import numpy as np
        DIM = 128
        DEPTH = 6
        HEADS = 16
        DIM_HEAD = 64
        WINDOW = 32
        INNER = HEADS * DIM_HEAD
        DIM_INNER = int(DIM * 4 * 2 / 3)
        QK_SCALE = 8.0

        def shift_tokens(t):
            a, s = jnp.split(t, 2, -1)
            s = jnp.pad(s, ((0, 0), (1, 0), (0, 0)))[:, :-1]
            return jnp.concatenate([a, s], -1)

        def l2norm(t):
            return t / jnp.maximum(jnp.linalg.norm(t, axis=-1, keepdims=True), 1e-12)

        def rotate_half(x):
            x1, x2 = jnp.split(x, 2, -1)
            return jnp.concatenate([-x2, x1], -1)

        def rotary_tables(n):
            half = jnp.arange(0, DIM_HEAD, 2, dtype=jnp.float32)
            inv_freq = 1.0 / 10000.0 ** (half / DIM_HEAD)
            t = jnp.arange(n, dtype=jnp.float32)
            freqs = t[:, None] * inv_freq[None, :]
            freqs = jnp.concatenate([freqs, freqs], -1)
            base_scale = (half + 0.4 * DIM_HEAD) / (1.4 * DIM_HEAD)
            power = (t - n // 2) / (WINDOW // 2)
            scale = base_scale[None, :] ** power[:, None]
            scale = jnp.concatenate([scale, scale], -1)
            return (freqs, scale)

        def local_attention(q, k, v):
            b, h, n, d = q.shape
            w = WINDOW
            nw = n // w
            bq = q.reshape(b, h, nw, w, d)
            bk = k.reshape(b, h, nw, w, d)
            bv = v.reshape(b, h, nw, w, d)

            def look(t):
                p = jnp.pad(t, ((0, 0), (0, 0), (1, 0), (0, 0), (0, 0)))
                return jnp.concatenate([p[:, :, :nw], p[:, :, 1:]], axis=3)
            bk2, bv2 = (look(bk), look(bv))
            seq = jnp.arange(n).reshape(nw, w)
            seq_p = jnp.pad(seq, ((1, 0), (0, 0)), constant_values=-1)
            jt = jnp.concatenate([seq_p[:nw], seq_p[1:]], axis=1)
            it = seq[:, :, None]
            jb = jt[:, None, :]
            mask = (it < jb) | (it > jb + w) | (jb == -1)
            sim = jnp.einsum('bhwie,bhwje->bhwij', bq, bk2) * QK_SCALE
            sim = jnp.where(mask, -jnp.finfo(sim.dtype).max, sim)
            attn = jax.nn.softmax(sim, -1)
            out = jnp.einsum('bhwij,bhwje->bhwie', attn, bv2)
            return out.reshape(b, h, n, d)

        def attn_layer(x, Wqkv, qs, ksc, Wo):
            b, n, _ = x.shape
            qkv = x @ Wqkv
            q, k, v = jnp.split(qkv, 3, -1)
            sh = lambda t: t.reshape(b, n, HEADS, DIM_HEAD).transpose(0, 2, 1, 3)
            q, k, v = (sh(q), sh(k), sh(v))
            q = l2norm(q) * qs
            k = l2norm(k) * ksc
            freqs, scale = rotary_tables(n)
            cos, sin = (jnp.cos(freqs), jnp.sin(freqs))
            q = q * cos * scale + rotate_half(q) * sin * scale
            inv = 1.0 / scale
            k = k * cos * inv + rotate_half(k) * sin * inv
            out = local_attention(q, k, v)
            out = out.transpose(0, 2, 1, 3).reshape(b, n, INNER)
            return out @ Wo

        def ffn_layer(x, g, bln, W1, b1, W2, b2):
            mu = x.mean(-1, keepdims=True)
            var = ((x - mu) ** 2).mean(-1, keepdims=True)
            xn = (x - mu) / jnp.sqrt(var + 1e-05) * g + bln
            hg = xn @ W1 + b1
            a, gate = jnp.split(hg, 2, -1)
            return a * jax.nn.gelu(gate, approximate=False) @ W2 + b2
        for i in range(DEPTH):
            x = attn_layer(shift_tokens(x), Wqkv[i], q_scale[i], k_scale[i], Wo[i]) + x
            x = ffn_layer(shift_tokens(x), ln_g[i], ln_b[i], W1[i], b1[i], W2[i], b2[i]) + x
        return x
    x = L0_attn_batch
    xn = _layernorm(x, axis=-1)
    s = _L0_attn_ref(xn, L0_attn_Wq, L0_attn_bq, L0_attn_Wk, L0_attn_bk, L0_attn_Wv, L0_attn_bv, L0_attn_Wo, L0_attn_bo)
    g = _silu(_L0_ffn_ref(xn, L0_ffn_ln1_w, L0_ffn_ln1_b, L0_ffn_ln2_w, L0_ffn_ln2_b, L0_ffn_conv_w, L0_ffn_attn_w, L0_ffn_proj_w, L0_ffn_router_w, L0_ffn_expert_wv, L0_ffn_expert_proj))
    x = x + s * g
    xn = _layernorm(x, axis=-1)
    s = _L1_attn_ref(xn, L1_attn_w_qkv, L1_attn_w_proj)
    g = _silu(_L1_ffn_ref(xn, L1_ffn_Wqkv, L1_ffn_q_scale, L1_ffn_k_scale, L1_ffn_Wo, L1_ffn_ln_g, L1_ffn_ln_b, L1_ffn_W1, L1_ffn_b1, L1_ffn_W2, L1_ffn_b2))
    x = x + s * g
    return x

_drawn_inputs = setup_inputs


def setup_inputs(seed=0):
    import zlib

    import numpy as np

    out = dict(_drawn_inputs(seed))
    spreads = {'L0_ffn_ln1_w': (1.0, 0.6),
     'L0_ffn_ln1_b': (0.0, 0.8),
     'L0_ffn_ln2_w': (1.0, 0.6),
     'L0_ffn_ln2_b': (0.0, 0.8),
     'L1_ffn_q_scale': (1.0, 0.6),
     'L1_ffn_k_scale': (1.0, 0.6),
     'L1_ffn_ln_g': (1.0, 0.6),
     'L1_ffn_ln_b': (0.0, 0.8),
     'L1_ffn_b1': (0.0, 0.8),
     'L1_ffn_b2': (0.0, 0.8)}
    factors = {'L0_attn_bq': 8.0,
     'L0_attn_bk': 64.0,
     'L0_attn_bv': 8.0,
     'L0_attn_bo': 8.0,
     'L0_ffn_conv_w': 8.0,
     'L0_ffn_attn_w': 8.0,
     'L0_ffn_proj_w': 8.0,
     'L0_ffn_router_w': 8.0,
     'L0_ffn_expert_wv': 8.0,
     'L0_ffn_expert_proj': 8.0,
     'L1_ffn_Wqkv': 2.985,
     'L1_ffn_Wo': 2.926,
     'L1_ffn_W1': 8.0,
     'L1_ffn_W2': 8.0}
    for name, (base, spread) in spreads.items():
        noise = np.random.default_rng([zlib.crc32(name.encode()), seed]).standard_normal(out[name].shape)
        drawn = base * np.exp(spread * noise) if base else spread * noise
        out[name] = jnp.asarray(drawn.astype(out[name].dtype))
    for name, factor in factors.items():
        out[name] = (out[name] * factor).astype(out[name].dtype)
    return out
```

```python
from contextlib import ExitStack

import numpy as np
import concourse.bass as bass
from concourse import mybir

ALU = mybir.AluOpType
ACT = mybir.ActivationFunctionType
AX_X = mybir.AxisListType.X
F32 = mybir.dt.float32
BF16 = mybir.dt.bfloat16

P = 128
C = 128
B = 4
L = 1024
T = B * L
CH = 512
NCH = T // CH
NT = T // P
TILES = L // P
QUAD = 32
EPS = 1e-5
MASKED = -1e30

HEADS = 16
HD = C // HEADS
HG = 4
GROUPS = HEADS // HG
PRODUCTS = ((0, 0), (0, 1), (0, 2), (1, 0), (1, 1), (2, 0))
STACK = len(PRODUCTS) * HD
SHIFT_ROW = 64
KROWS = SHIFT_ROW + 2

E = 4
DFF = 512

LAYERS = 6
DH = 64
INNER = HEADS * DH
PAIRS = HEADS // 2
WIN = 32
SPAN = P + WIN
DI = int(C * 4 * 2 / 3)
DCH = [(o, min(P, DI - o)) for o in range(0, DI, P)]
QK_SCALE = 8.0

FIRST_SEM = 150


class Stage:

    def __init__(self, nc, name):
        self.nc, self.name, self.ctx, self.sems = nc, name, ExitStack(), []

    def __enter__(self):
        return self

    def __exit__(self, kind, *rest):
        if kind is None and self.sems:
            self.nc.all_engine_barrier(sems_to_clear=range(FIRST_SEM, FIRST_SEM + len(self.sems)))
        self.ctx.close()
        return False

    def sem(self, name):
        number = FIRST_SEM + len(self.sems)
        self.sems.append(self.ctx.enter_context(self.nc.semaphore(f"{self.name}_{name}", num=number)))
        return self.sems[-1]

    def sb(self, name, shape, dt=F32):
        return self.ctx.enter_context(self.nc.sbuf_tensor(f"{name}_of_{self.name}", shape, dt))


class Chain:

    def __init__(self, eng, sem):
        self.eng, self.sem, self.n = eng, sem, 0

    def __call__(self, ins):
        self.n += 1
        ins.then_inc(self.sem, 1)
        self.eng.wait_ge(self.sem, self.n)


def chunk(c):
    return slice(c * CH, (c + 1) * CH)


def load_constants(nc, pairs):
    with Stage(nc, "load") as st:
        loaded = st.sem("loaded")
        with nc.Block() as block:

            @block.sync
            def _(sp):
                for dst, src in pairs:
                    sp.dma_start(dst, src).then_inc(loaded, 16)
                sp.wait_ge(loaded, 16 * len(pairs))


def layernorm(nc, name, ps, k, src, dst, weight=None, bias=None):
    with Stage(nc, name) as st:
        square = st.sb("square", [P, 4, CH])
        rstd = st.sb("rstd", [P, CH])
        mean_ready, centred, squared = st.sem("mean_ready"), st.sem("centred"), st.sem("squared")
        var_part, var_eps, rooted = st.sem("var_part"), st.sem("var_eps"), st.sem("rooted")
        inverse, spread, scaled, done = st.sem("inverse"), st.sem("spread"), st.sem("scaled"), st.sem("done")
        with nc.Block() as block:

            @block.tensor
            def _(pe):
                for c in range(NCH):
                    if c >= 4:
                        pe.wait_ge(centred, c - 3)
                    nc.tensor.matmul(ps[:, c % 4, :], k["mean"][:, :], src[:, chunk(c)],
                                     start=True, stop=True).then_inc(mean_ready, 1)
                for c in range(NCH):
                    pe.wait_ge(squared, c + 1)
                    q = c % 4 * QUAD
                    nc.tensor.matmul(ps[q:q + QUAD, 4, :], k["mean_row"][:, c // 4, :], square[:, c % 4, :],
                                     start=c < 4, stop=c >= 4).then_inc(var_part, 1)
                pe.wait_ge(inverse, 1)
                for c in range(NCH):
                    if c >= 4:
                        pe.wait_ge(scaled, c - 3)
                    nc.tensor.matmul(ps[:, c % 4, :], k["pick_row"][:, c, :], rstd[:, :],
                                     start=True, stop=True).then_inc(spread, 1)

            @block.scalar
            def _(act):
                for c in range(NCH):
                    act.wait_ge(centred, c + 1)
                    if c >= 4:
                        act.wait_ge(var_part, c - 3)
                    nc.scalar.activation(square[:, c % 4, :], dst[:, chunk(c)], ACT.Square).then_inc(squared, 1)
                act.wait_ge(var_eps, 1)
                nc.scalar.activation(rstd[:, :], rstd[:, :], ACT.Sqrt).then_inc(rooted, 1)
                if weight is not None:
                    for c in range(NCH):
                        act.wait_ge(scaled, c + 1)
                        nc.scalar.activation(dst[:, chunk(c)], dst[:, chunk(c)], ACT.Identity,
                                             bias=bias, scale=weight).then_inc(done, 1)
                    act.wait_ge(done, NCH)

            @block.vector
            def _(dve):
                for c in range(NCH):
                    dve.wait_ge(mean_ready, c + 1)
                    nc.vector.tensor_tensor(dst[:, chunk(c)], src[:, chunk(c)], ps[:, c % 4, :],
                                            ALU.subtract).then_inc(centred, 1)
                dve.wait_ge(var_part, NCH)
                nc.vector.tensor_scalar(rstd[:, :], ps[:, 4, :], EPS, None, ALU.add).then_inc(var_eps, 1)
                dve.wait_ge(rooted, 1)
                nc.vector.reciprocal(rstd[:, :], rstd[:, :]).then_inc(inverse, 1)
                for c in range(NCH):
                    dve.wait_ge(spread, c + 1)
                    if c == 0:
                        dve.wait_ge(squared, NCH)
                    nc.vector.tensor_tensor(dst[:, chunk(c)], dst[:, chunk(c)], ps[:, c % 4, :],
                                            ALU.mult).then_inc(scaled, 1)
                dve.wait_ge(scaled, NCH)


def tile_attention(nc, ps, k, w, xn, out):
    scale = float(1.0 / np.sqrt(C))
    with nc.Fori(0, B) as b, Stage(nc, "ta") as st:
        x = st.sb("x", [P, L])
        qT = st.sb("qT", [P, L])
        kT = st.sb("kT", [P, L])
        v = st.sb("v", [P, TILES, P])
        prob = st.sb("prob", [P, 2, TILES, P])
        probT = st.sb("probT", [P, 2, TILES, P])
        outT = st.sb("outT", [P, 2, CH])
        top = st.sb("top", [P, TILES])
        total = st.sb("total", [P, 2, TILES])
        norm = st.sb("norm", [P, 1])
        got_x, projected, biased, v_ready = st.sem("got_x"), st.sem("projected"), st.sem("biased"), st.sem("v_ready")
        scored, shifted, raised, weighed = st.sem("scored"), st.sem("shifted"), st.sem("raised"), st.sem("weighed")
        turned, turned_out, summed, evened = st.sem("turned"), st.sem("turned_out"), st.sem("summed"), st.sem("evened")
        mixed, written, chain = st.sem("mixed"), st.sem("written"), st.sem("chain")
        with nc.Block() as block:

            @block.tensor
            def _(pe):
                pe.wait_ge(got_x, 1)
                for h in range(2):
                    for n, name in enumerate(("ta_q", "ta_k")):
                        nc.tensor.matmul(ps[:, 2 * n + h, :], w[name][:, :], x[:, chunk(h)],
                                         start=True, stop=True).then_inc(projected, 1)
                for t in range(TILES):
                    nc.tensor.matmul(ps[:, 4 + t // 4, t % 4 * P:(t % 4 + 1) * P], x[:, t * P:(t + 1) * P],
                                     w["ta_v"][:, :], start=True, stop=True).then_inc(projected, 1)
                pe.wait_ge(biased, 4)

                def score(t):
                    if t >= 2:
                        pe.wait_ge(shifted, t - 1)
                    for h in range(2):
                        last = nc.tensor.matmul(ps[:, t % 2 * 2 + h, :], qT[:, t * P:(t + 1) * P], kT[:, chunk(h)],
                                                start=True, stop=True)
                    last.then_inc(scored, 1)

                def turn(t):
                    pe.wait_ge(weighed, t + 1)
                    if t >= 1:
                        pe.wait_ge(turned_out, t)
                    else:
                        pe.wait_ge(v_ready, 2)
                    for j in range(TILES):
                        last = nc.tensor.transpose(ps[:, 4 + j // 4, j % 4 * P:(j % 4 + 1) * P],
                                                   prob[:, t % 2, j, :], k["ident"][:, :])
                    last.then_inc(turned, 1)

                def gather(t):
                    pe.wait_ge(turned_out, t + 1)
                    if t == 4:
                        pe.wait_ge(evened, 1)
                    for j in range(TILES):
                        last = nc.tensor.matmul(ps[:, 6, t % 4 * P:(t % 4 + 1) * P], v[:, j, :],
                                                probT[:, t % 2, j, :], start=j == 0, stop=j == TILES - 1)
                    last.then_inc(summed, 1)

                def mix(h):
                    pe.wait_ge(evened, h + 1)
                    if h:
                        pe.wait_ge(written, 1)
                    nc.tensor.matmul(ps[:, 7, :], w["ta_o"][:, :], outT[:, h, :], start=True,
                                     stop=True).then_inc(mixed, 1)

                score(0)
                for t in range(TILES):
                    if t + 1 < TILES:
                        score(t + 1)
                    turn(t)
                    gather(t)
                    if t == 4:
                        mix(0)
                mix(1)

            @block.scalar
            def _(act):
                for h in range(2):
                    for n, (dst, bias) in enumerate(((qT, "ta_bq"), (kT, "ta_bk"))):
                        act.wait_ge(projected, 2 * h + n + 1)
                        nc.scalar.activation(dst[:, chunk(h)], ps[:, 2 * n + h, :], ACT.Identity,
                                             bias=w[bias][:, :]).then_inc(biased, 1)

                def copy_out(t):
                    act.wait_ge(turned, t + 1)
                    if t >= 2:
                        act.wait_ge(summed, t - 1)
                    nc.scalar.activation(probT[:, t % 2].rearrange("p j q -> p (j q)"),
                                         ps[:, 4:6, :].rearrange("p a n -> p (a n)"), ACT.Copy).then_inc(turned_out, 1)

                def finish(h):
                    act.wait_ge(mixed, h + 1)
                    nc.scalar.activation(out[:, bass.ds(b * L + h * CH, CH)], ps[:, 7, :], ACT.Identity,
                                         bias=w["ta_bo"][:, :]).then_inc(written, 1)

                for t in range(TILES):
                    act.wait_ge(shifted, t + 1)
                    nc.scalar.activation(prob[:, t % 2], prob[:, t % 2], ACT.Exp, scale=scale).then_inc(raised, 1)
                    if t >= 1:
                        copy_out(t - 1)
                    if t == 6:
                        finish(0)
                copy_out(TILES - 1)
                finish(1)
                act.wait_ge(written, 2)

            @block.vector
            def _(dve):
                link = Chain(dve, chain)
                nc.vector.tensor_copy(x[:, :], xn[:, bass.ds(b * L, L)]).then_inc(got_x, 1)
                dve.wait_ge(projected, 12)
                for a in range(2):
                    nc.vector.tensor_tensor(v[:, 4 * a:4 * a + 4, :], ps[:, 4 + a, :].rearrange("p (t n) -> p t n", n=P),
                                            w["ta_bv"][:, :].unsqueeze(1).to_broadcast([P, 4, P]),
                                            ALU.add).then_inc(v_ready, 1)

                def shift(t):
                    s = ps[:, t % 2 * 2:t % 2 * 2 + 2, :].rearrange("p a (j n) -> p (a j) n", n=P)
                    dve.wait_ge(scored, t + 1)
                    if t >= 1:
                        dve.wait_ge(shifted, t)
                    link(nc.vector.reduce_max(top[:, :], s, AX_X))
                    if t >= 2:
                        dve.wait_ge(turned, t - 1)
                    nc.vector.tensor_tensor(prob[:, t % 2], s, top[:, :].unsqueeze(2).to_broadcast([P, TILES, P]),
                                            ALU.subtract).then_inc(shifted, 1)

                def weigh(t):
                    a, r = total[:, 0, :], total[:, 1, :]
                    dve.wait_ge(raised, t + 1)
                    if t >= 1:
                        dve.wait_ge(weighed, t)
                    link(nc.vector.reduce_sum(a, prob[:, t % 2], AX_X))
                    link(nc.vector.reciprocal(r, a))
                    link(nc.vector.tensor_tensor(a, a, r, ALU.mult))
                    link(nc.vector.reduce_sum(norm[:, :], a, AX_X))
                    link(nc.vector.tensor_scalar(norm[:, :], norm[:, :], 1e-6, None, ALU.add))
                    link(nc.vector.reciprocal(norm[:, :], norm[:, :]))
                    link(nc.vector.tensor_scalar(r, r, norm[:, :], None, ALU.mult))
                    nc.vector.tensor_tensor(prob[:, t % 2], prob[:, t % 2],
                                            r.unsqueeze(2).to_broadcast([P, TILES, P]), ALU.mult).then_inc(weighed, 1)

                def even(h):
                    dve.wait_ge(summed, 4 * h + 4)
                    nc.vector.tensor_copy(outT[:, h, :], ps[:, 6, :]).then_inc(evened, 1)

                shift(0)
                for t in range(TILES):
                    if t + 1 < TILES:
                        shift(t + 1)
                    if t == 4:
                        even(0)
                    weigh(t)
                even(1)
                dve.wait_ge(evened, 2)


def causal_convolution(nc, taps, h, out):
    with Stage(nc, "conv") as st:
        chain = st.sem("chain")
        hv = h[:, :].rearrange("p (b t) -> p b t", b=B)
        ov = out[:, :].rearrange("p (b t) -> p b t", b=B)
        with nc.Block() as block:

            @block.vector
            def _(dve):
                link = Chain(dve, chain)
                link(nc.vector.tensor_scalar(ov, hv, taps[:, 2:3], None, ALU.mult))
                for back in (1, 2):
                    link(nc.vector.scalar_tensor_tensor(out=ov[:, :, back:], in0=hv[:, :, :L - back],
                                                        scalar=taps[:, 2 - back:3 - back], in1=ov[:, :, back:],
                                                        op0=ALU.mult, op1=ALU.add))


def causal_inputs(nc, name, ps, h, weights, tables, q_parts, k_parts, vtok):
    rotated = tables is not None
    with Stage(nc, name) as st:
        value = st.sb("value", [P, 2, CH])
        sine = st.sb("sine", [P, 2, CH])
        rest = st.sb("rest", [P, 2, CH])
        parts = st.sb("parts", [P, 4, 3, CH], BF16)
        projected, v_projected, bank_used = st.sem("projected"), st.sem("v_projected"), st.sem("bank_used")
        valued, high, rested, middle, low = (st.sem(n) for n in ("valued", "high", "rested", "middle", "low"))
        stored, v_out, chain = [st.sem(f"stored{n}") for n in range(4)], st.sem("v_out"), st.sem("chain")
        again = st.sem("again")
        with nc.Block() as block:

            @block.tensor
            def _(pe):
                for c in range(NCH):
                    for n in range(2):
                        i = 2 * c + n
                        if c:
                            pe.wait_ge(bank_used, i - 1)
                        last = nc.tensor.matmul(ps[:, 2 * n, :], weights["qk"[n]][:, :], h[:, chunk(c)],
                                                start=True, stop=True)
                        if rotated:
                            last = nc.tensor.matmul(ps[:, 2 * n + 1, :], weights["qk"[n] + "_swapped"][:, :],
                                                    h[:, chunk(c)], start=True, stop=True)
                        last.then_inc(projected, 1)
                    if c >= 2:
                        pe.wait_ge(v_out, c - 1)
                    for t in range(4):
                        a = c * CH + t * P
                        last = nc.tensor.matmul(ps[:, 4 + c % 2, t * P:(t + 1) * P], h[:, a:a + P], weights["v"][:, :],
                                                start=True, stop=True)
                    last.then_inc(v_projected, 1)

            @block.vector
            def _(dve):
                for c in range(NCH):
                    for n in range(2):
                        i, slot = 2 * c + n, c % 2 * 2 + n
                        dve.wait_ge(projected, i + 1)
                        if i >= 2:
                            dve.wait_ge(high, i - 1)
                            dve.wait_ge(rested, i - 1)
                        if rotated:
                            at = slice(c % 2 * CH, (c % 2 + 1) * CH)
                            nc.vector.tensor_tensor(value[:, n, :], ps[:, 2 * n, :], tables["cos"][:, at],
                                                    ALU.mult).then_inc(chain, 1)
                            if i >= 2:
                                dve.wait_ge(valued, i - 1)
                            nc.vector.tensor_tensor(sine[:, n, :], ps[:, 2 * n + 1, :], tables["sin"][:, at],
                                                    ALU.mult).then_inc(bank_used, 1)
                            dve.wait_ge(bank_used, i + 1)
                            dve.wait_ge(chain, i + 1)
                            nc.vector.tensor_tensor(value[:, n, :], value[:, n, :], sine[:, n, :],
                                                    ALU.add).then_inc(valued, 1)
                        else:
                            nc.vector.tensor_copy(value[:, n, :], ps[:, 2 * n, :]).then_inc(valued, 1)
                            dve.wait_ge(valued, i + 1)
                            dve.sem_inc(bank_used, 1)
                        dve.wait_ge(valued, i + 1)
                        dve.wait_ge(high, i + 1)
                        if i >= 2:
                            dve.wait_ge(low, i - 1)
                            dve.wait_ge(middle, i - 1)
                        nc.vector.tensor_tensor(rest[:, n, :], value[:, n, :], parts[:, slot, 0, :],
                                                ALU.subtract).then_inc(rested, 1)
                        dve.wait_ge(middle, i + 1)
                        nc.vector.tensor_tensor(parts[:, slot, 2, :], rest[:, n, :], parts[:, slot, 1, :],
                                                ALU.subtract).then_inc(low, 1)
                dve.wait_ge(low, 2 * NCH)

            @block.scalar
            def _(act):
                for c in range(NCH):
                    for n in range(2):
                        i, slot = 2 * c + n, c % 2 * 2 + n
                        act.wait_ge(valued, i + 1)
                        if c >= 2:
                            act.wait_ge(stored[slot], 16 * (c // 2))
                            act.wait_ge(again, 16 * min(2 * (c - 2) + n + 1, 2 * L // CH))
                        nc.scalar.activation(parts[:, slot, 0, :], value[:, n, :], ACT.Copy).then_inc(high, 1)
                        act.wait_ge(rested, i + 1)
                        nc.scalar.activation(parts[:, slot, 1, :], rest[:, n, :], ACT.Copy).then_inc(middle, 1)
                    act.wait_ge(v_projected, c + 1)
                    nc.scalar.activation(vtok[:, 4 * c:4 * c + 4, :], ps[:, 4 + c % 2, :].rearrange("p (t n) -> p t n", n=P),
                                         ACT.Copy).then_inc(v_out, 1)
                act.wait_ge(v_out, NCH)

            @block.sync
            def _(sp):
                for c in range(NCH):
                    for n, dram in enumerate((q_parts, k_parts)):
                        slot = c % 2 * 2 + n
                        sp.wait_ge(low, 2 * c + n + 1)
                        sp.dma_start(dram[:, :, chunk(c)].rearrange("s p t -> p s t"),
                                     parts[:, slot]).then_inc(stored[slot], 16)
                        if c < L // CH:
                            sp.dma_start(dram[:, :, chunk(NCH + c)].rearrange("s p t -> p s t"),
                                         parts[:, slot]).then_inc(again, 16)
                            sp.wait_ge(again, 16 * (2 * c + n + 1))
                for slot in range(4):
                    sp.wait_ge(stored[slot], 16 * (NCH // 2))


UNITS = [(qc, kt, max(0, kt - qc * 4) * P) for qc in range(2) for kt in range(4 * qc + 4)]
PIECES = [(h, qt, lo, min(CH, (qt + 1) * P - lo)) for h in range(HG) for qt in range(TILES)
          for lo in range(0, (qt + 1) * P, CH)]
PER_HEAD = len(PIECES) // HG


class Maxima:

    def __init__(self, nc, st, ps, k, stack, buf):
        self.nc, self.ps, self.k, self.stack, self.buf = nc, ps, k, stack, buf
        self.scored, self.used, self.neg = st.sem("max_scored"), st.sem("max_used"), st.sem("max_neg")
        self.rows, self.rows_out, self.placed = st.sem("max_rows"), st.sem("max_rows_out"), st.sem("max_placed")

    def pe_piece(self, pe, i):
        nc, ps, (queries, keys) = self.nc, self.ps, self.stack
        h, qt, lo, n = PIECES[i]
        bank, diagonal = 5 + i % 3, lo + n == (qt + 1) * P
        if i >= 3:
            pe.wait_ge(self.used, i - 2)
        last = nc.tensor.matmul(ps[:, bank, 0:n], queries[0:STACK, h, qt * P:(qt + 1) * P], keys[0:STACK, h, lo:lo + n],
                                start=True, stop=not diagonal)
        if diagonal:
            last = nc.tensor.matmul(ps[:, bank, n - P:n], self.k["ident_b"][:, :], self.k["after_q"][:, :],
                                    start=False, stop=True)
        last.then_inc(self.scored, 1)

    def pe_rows(self, pe):
        nc, ps = self.nc, self.ps
        pe.wait_ge(self.neg, 6)
        for qt in range(TILES):
            last = nc.tensor.matmul(ps[0:2 * HG, 5 + qt // 4, qt % 4 * P:(qt % 4 + 1) * P],
                                    self.buf["neg_parts"][:, qt].rearrange("p h s -> p (h s)"), self.k["ident_b"][:, :],
                                    start=True, stop=True)
        last.then_inc(self.rows, 1)

    def dve_piece(self, dve, i):
        h, qt, lo, n = PIECES[i]
        dve.wait_ge(self.scored, i + 1)
        self.nc.vector.reduce_max(self.buf["top"][:, h, i % PER_HEAD:i % PER_HEAD + 1], self.ps[:, 5 + i % 3, 0:n],
                                  AX_X).then_inc(self.used, 1)

    def dve_rows(self, dve):
        nc, top, neg, parts = self.nc, self.buf["top"], self.buf["neg"], self.buf["neg_parts"]
        dve.wait_ge(self.used, len(PIECES))
        link = Chain(dve, self.neg)
        half = TILES // 2
        late = top[:, :, half:].rearrange("p h (t s) -> p h t s", s=2)
        link(nc.vector.tensor_tensor(neg[:, :, half:], late[:, :, :, 0], late[:, :, :, 1], ALU.max))
        link(nc.vector.tensor_scalar(neg[:, :, half:], neg[:, :, half:], -1.0, None, ALU.mult))
        link(nc.vector.tensor_scalar(neg[:, :, :half], top[:, :, :half], -1.0, None, ALU.mult))
        turned = neg[:, :, :].rearrange("p h t -> p t h")
        link(nc.vector.tensor_copy(parts[:, :, :, 0], turned))
        link(nc.vector.tensor_tensor(turned, turned, parts[:, :, :, 0], ALU.subtract))
        link(nc.vector.tensor_copy(parts[:, :, :, 1], turned))
        dve.wait_ge(self.rows, 1)
        nc.vector.tensor_copy(self.buf["rows"][:, :], self.ps[0:2 * HG, 5:7, :].rearrange("p a n -> p (a n)"))\
            .then_inc(self.rows_out, 1)

    def sp_rows(self, sp):
        sp.wait_ge(self.rows_out, 1)
        for h in range(HG):
            sp.dma_start(self.stack[0][SHIFT_ROW:SHIFT_ROW + 2, h, :], self.buf["rows"][2 * h:2 * h + 2, :])\
                .then_inc(self.placed, 16)
        sp.wait_ge(self.placed, 16 * HG)


def load_stack(sp, sem, stack, q_parts, k_parts, first, group):
    for side, (dst, dram) in enumerate(zip(stack, (q_parts, k_parts))):
        for r, pair in enumerate(PRODUCTS):
            src = dram[pair[side], group * HG * HD:(group + 1) * HG * HD, bass.ds(first, L)]
            sp.dma_start(dst[r * HD:(r + 1) * HD, :, :], src.rearrange("(h d) t -> d h t", d=HD)).then_inc(sem, 16)
    return 16 * 2 * len(PRODUCTS)


def causal_attention(nc, name, ps, k, q_parts, k_parts, vtok, proj, out, residual):
    scale = float(1.0 / np.sqrt(HD))
    with ExitStack() as ctx:
        sb = lambda n, shape, dt=F32: ctx.enter_context(nc.sbuf_tensor(f"{n}_of_{name}", shape, dt))
        stacks = [(sb(f"queries{s}", [P, HG, L], BF16), sb(f"keys{s}", [P, HG, L], BF16)) for s in range(GROUPS)]
        prob = sb("prob", [P, 2, HG, CH])
        values = sb("values", [P, TILES, HG, QUAD])
        summed = sb("summed", [P, 2, GROUPS, CH])
        inverse = sb("inverse", [QUAD, CH])
        evened = sb("evened", [P, 2, CH])
        buf = dict(top=sb("top", [P, HG, PER_HEAD]), neg=sb("neg", [P, HG, TILES]),
                   neg_parts=sb("neg_parts", [P, TILES, HG, 2], BF16), rows=sb("rows", [2 * HG, L], BF16))

        with Stage(nc, name + "_first") as st:
            cleared, loaded = st.sem("cleared"), st.sem("loaded")
            maxima = Maxima(nc, st, ps, k, stacks[0], buf)
            with nc.Block() as block:

                @block.gpsimd
                def _(pool):
                    link = Chain(pool, cleared)
                    for q, kk in stacks:
                        link(nc.gpsimd.memset(q[QUAD:SHIFT_ROW, :, :], 0.0))
                        link(nc.gpsimd.memset(kk[QUAD:SHIFT_ROW, :, :], 0.0))
                        link(nc.gpsimd.memset(kk[SHIFT_ROW:SHIFT_ROW + 2, :, :], 1.0))
                    link(nc.gpsimd.memset(values[:, :, :, HD:], 0.0))
                    link(nc.gpsimd.memset(values[:, :, :, HD:HD + 1], 1.0))

                @block.sync
                def _(sp):
                    sp.wait_ge(cleared, 3 * GROUPS + 2)
                    for g in range(2):
                        n = load_stack(sp, loaded, stacks[g], q_parts, k_parts, 0, g)
                    sp.wait_ge(loaded, 2 * n)
                    maxima.sp_rows(sp)

                @block.tensor
                def _(pe):
                    pe.wait_ge(loaded, 2 * 16 * 2 * len(PRODUCTS))
                    for i in range(len(PIECES)):
                        maxima.pe_piece(pe, i)
                    maxima.pe_rows(pe)

                @block.vector
                def _(dve):
                    for i in range(len(PIECES)):
                        maxima.dve_piece(dve, i)
                    maxima.dve_rows(dve)

        with nc.Fori(0, B) as b:
            for g in range(GROUPS):
                with Stage(nc, f"{name}_g{g}") as st:
                    queries, keys = stacks[g]
                    placed, loaded = st.sem("placed"), st.sem("loaded")
                    scored, raised, weighed, acc_out = (st.sem(n) for n in ("scored", "raised", "weighed", "acc_out"))
                    maxima = Maxima(nc, st, ps, k, stacks[(g + 1) % GROUPS], buf)
                    with nc.Block() as block:

                        @block.sync
                        def _(sp):
                            ahead = g + 2
                            n = load_stack(sp, loaded, stacks[ahead % GROUPS], q_parts, k_parts,
                                           (b + ahead // GROUPS) * L, ahead % GROUPS)
                            maxima.sp_rows(sp)
                            sp.wait_ge(loaded, n)

                        @block.gpsimd
                        def _(pool):
                            src = vtok[:, bass.ds(b * TILES, TILES), g * HG * HD:(g + 1) * HG * HD]
                            nc.gpsimd.tensor_copy(values[:, :, :, 0:HD], src.rearrange("p t (h d) -> p t h d", d=HD))\
                                .then_inc(placed, 1)
                            pool.wait_ge(placed, 1)

                        @block.tensor
                        def _(pe):
                            def score(i):
                                qc, kt, j = UNITS[i]
                                diagonal = kt >= 4 * qc
                                for pair in range(2):
                                    if i:
                                        pe.wait_ge(raised, 2 * i - 1 + pair)
                                    for h in (2 * pair, 2 * pair + 1):
                                        last = nc.tensor.matmul(ps[:, h, j:], keys[0:KROWS, h, kt * P:(kt + 1) * P],
                                                                queries[0:KROWS, h, qc * CH + j:(qc + 1) * CH],
                                                                start=True, stop=not diagonal)
                                        if diagonal:
                                            last = nc.tensor.matmul(ps[:, h, j:j + P], k["ident_b"][:, :],
                                                                    k["after_k"][:, :], start=False, stop=True)
                                    last.then_inc(scored, 1)

                            def weigh(i):
                                qc, kt, j = UNITS[i]
                                pe.wait_ge(raised, 2 * i + 2)
                                if i == 0:
                                    pe.wait_ge(placed, 1)
                                if qc == 1 and kt == 0:
                                    pe.wait_ge(acc_out, 1)
                                for h in range(HG):
                                    last = nc.tensor.matmul(ps[h * QUAD:(h + 1) * QUAD, 4, j:], values[:, kt, h, :],
                                                            prob[:, i % 2, h, j:], start=kt == 0, stop=kt == 4 * qc + 3)
                                last.then_inc(weighed, 1)

                            score(0)
                            for i in range(len(UNITS)):
                                if i + 1 < len(UNITS):
                                    score(i + 1)
                                weigh(i)
                                for n in range(HG):
                                    maxima.pe_piece(pe, HG * i + n)
                            maxima.pe_rows(pe)

                        @block.scalar
                        def _(act):
                            for i, (qc, kt, j) in enumerate(UNITS):
                                for pair in range(2):
                                    act.wait_ge(scored, 2 * i + pair + 1)
                                    if i >= 2:
                                        act.wait_ge(weighed, i - 1)
                                    nc.scalar.activation(prob[:, i % 2, 2 * pair:2 * pair + 2, j:],
                                                         ps[:, 2 * pair:2 * pair + 2, j:], ACT.Exp,
                                                         scale=scale).then_inc(raised, 1)

                        @block.vector
                        def _(dve):
                            for i in range(len(UNITS)):
                                for n in range(HG):
                                    maxima.dve_piece(dve, HG * i + n)
                                if i in (3, len(UNITS) - 1):
                                    half = int(i > 3)
                                    dve.wait_ge(weighed, (4, len(UNITS))[half])
                                    nc.vector.tensor_copy(summed[:, half, g, :], ps[:, 4, :]).then_inc(acc_out, 1)
                            maxima.dve_rows(dve)
                            dve.wait_ge(acc_out, 2)

            with Stage(nc, name + "_project") as st:
                totals, inverted, spread, even, projected, done = (
                    st.sem(n) for n in ("totals", "inverted", "spread", "even", "projected", "done"))
                units = [(half, g) for half in range(2) for g in range(GROUPS)]
                with nc.Block() as block:

                    @block.tensor
                    def _(pe):
                        for u, (half, g) in enumerate(units):
                            last = nc.tensor.matmul(ps[0:QUAD, 0, :], k["pick_total"][:, u, :], summed[:, half, g, :],
                                                    start=u == 0, stop=u == len(units) - 1)
                        last.then_inc(totals, 1)
                        pe.wait_ge(inverted, 1)

                        def mix(u):
                            half, g = units[u]
                            pe.wait_ge(even, u + 1)
                            nc.tensor.matmul(ps[:, 4 + half, :], proj[:, g, :], evened[:, u % 2, :],
                                             start=g == 0, stop=g == GROUPS - 1).then_inc(projected, 1)

                        for u in range(len(units)):
                            if u >= 2:
                                pe.wait_ge(even, u - 1)
                            nc.tensor.matmul(ps[:, 2 + u % 2, :], k["spread_total"][:, u, :], inverse[:, :],
                                             start=True, stop=True).then_inc(spread, 1)
                            if u:
                                mix(u - 1)
                        mix(len(units) - 1)

                    @block.vector
                    def _(dve):
                        dve.wait_ge(totals, 1)
                        nc.vector.reciprocal(inverse[:, :], ps[0:QUAD, 0, :]).then_inc(inverted, 1)
                        for u, (half, g) in enumerate(units):
                            dve.wait_ge(spread, u + 1)
                            if u >= 2:
                                dve.wait_ge(projected, u - 1)
                            nc.vector.tensor_tensor(evened[:, u % 2, :], summed[:, half, g, :], ps[:, 2 + u % 2, :],
                                                    ALU.mult).then_inc(even, 1)
                        for half in range(2):
                            at = bass.ds(b * L + half * CH, CH)
                            dve.wait_ge(projected, GROUPS * (half + 1))
                            if residual is not None:
                                nc.vector.tensor_tensor(out[:, at], ps[:, 4 + half, :], residual[:, at],
                                                        ALU.add).then_inc(done, 1)
                            else:
                                nc.vector.tensor_copy(out[:, at], ps[:, 4 + half, :]).then_inc(done, 1)
                        dve.wait_ge(done, 2)


def route(nc, ps, router, h, mask):
    with Stage(nc, "route") as st:
        logits, best, taken = st.sb("logits", [P, NT, E]), st.sb("best", [P, NT]), st.sb("taken", [P, NT])
        scored, chain = st.sem("scored"), st.sem("chain")
        with nc.Block() as block:

            @block.tensor
            def _(pe):
                for t in range(NT):
                    last = nc.tensor.matmul(ps[:, 0, t * E:(t + 1) * E], h[:, t * P:(t + 1) * P], router[:, :],
                                            start=True, stop=True)
                last.then_inc(scored, 1)

            @block.vector
            def _(dve):
                link = Chain(dve, chain)
                dve.wait_ge(scored, 1)
                link(nc.vector.tensor_copy(logits[:, :, :], ps[:, 0, 0:NT * E].rearrange("p (t e) -> p t e", e=E)))
                link(nc.vector.reduce_max(best[:, :], logits[:, :, :], AX_X))
                link(nc.vector.tensor_tensor(logits[:, :, :], logits[:, :, :],
                                             best[:, :].unsqueeze(2).to_broadcast([P, NT, E]), ALU.is_equal))
                link(nc.vector.tensor_copy(mask[:, :, 0], logits[:, :, 0]))
                link(nc.vector.tensor_copy(taken[:, :], logits[:, :, 0]))
                for e in range(1, E):
                    link(nc.vector.tensor_tensor(mask[:, :, e], logits[:, :, e], taken[:, :], ALU.is_gt))
                    link(nc.vector.tensor_tensor(taken[:, :], taken[:, :], logits[:, :, e], ALU.max))


def experts(nc, ps, k, wv, wp, h, mask, xa, s, x):
    FCH = DFF // P
    units = [(e, f) for e in range(E) for f in range(FCH)]
    with nc.Fori(0, NCH) as c, Stage(nc, "moe") as st:
        own = st.sb("own", [P, E, CH])
        gate = st.sb("gate", [P, 2, CH])
        act_v = st.sb("gated", [P, 2, CH])
        total = st.sb("total", [P, CH])
        spread, masked, gates, vals = (st.sem(n) for n in ("spread", "masked", "gates", "vals"))
        silus, gated, summed, chain, silu2 = (st.sem(n) for n in ("silus", "gated", "summed", "chain", "silu2"))
        with nc.Block() as block:

            @block.tensor
            def _(pe):
                for e in range(E):
                    if e >= 2:
                        pe.wait_ge(masked, e - 1)
                    for t in range(4):
                        col = mask[:, bass.ds(c * 4 + t, 1), e]
                        last = nc.tensor.matmul(ps[:, 6 + e % 2, t * P:(t + 1) * P], col.to_broadcast([P, P]),
                                                k["ident_b"][:, :], start=True, stop=True)
                    last.then_inc(spread, 1)

                def down(u):
                    e, f = units[u]
                    pe.wait_ge(gated, u + 1)
                    nc.tensor.matmul(ps[:, 4, :], wp[:, e, f, :], act_v[:, u % 2, :], start=u == 0,
                                     stop=u == len(units) - 1).then_inc(summed, 1)

                for u, (e, f) in enumerate(units):
                    pe.wait_ge(masked, e + 1)
                    if u >= 2:
                        pe.wait_ge(gated, u - 1)
                    nc.tensor.matmul(ps[:, u % 2, :], wv[:, e, f * P:(f + 1) * P], own[:, e, :],
                                     start=True, stop=True).then_inc(gates, 1)
                    nc.tensor.matmul(ps[:, 2 + u % 2, :], wv[:, e, DFF + f * P:DFF + (f + 1) * P], own[:, e, :],
                                     start=True, stop=True).then_inc(vals, 1)
                    if u:
                        down(u - 1)
                down(len(units) - 1)

            @block.scalar
            def _(act):
                for u in range(len(units)):
                    act.wait_ge(gates, u + 1)
                    if u >= 2:
                        act.wait_ge(gated, u - 1)
                    nc.scalar.activation(gate[:, u % 2, :], ps[:, u % 2, :], ACT.Silu).then_inc(silus, 1)
                act.wait_ge(chain, 1)
                nc.scalar.activation(total[:, :], total[:, :], ACT.Silu).then_inc(silu2, 1)

            @block.vector
            def _(dve):
                for e in range(E):
                    dve.wait_ge(spread, e + 1)
                    nc.vector.tensor_tensor(own[:, e, :], h[:, bass.ds(c * CH, CH)], ps[:, 6 + e % 2, :],
                                            ALU.mult).then_inc(masked, 1)
                for u in range(len(units)):
                    dve.wait_ge(silus, u + 1)
                    dve.wait_ge(vals, u + 1)
                    if u >= 2:
                        dve.wait_ge(summed, u - 1)
                    nc.vector.tensor_tensor(act_v[:, u % 2, :], gate[:, u % 2, :], ps[:, 2 + u % 2, :],
                                            ALU.mult).then_inc(gated, 1)
                at = bass.ds(c * CH, CH)
                dve.wait_ge(summed, len(units))
                nc.vector.tensor_tensor(total[:, :], xa[:, at], ps[:, 4, :], ALU.add).then_inc(chain, 1)
                dve.wait_ge(silu2, 1)
                nc.vector.tensor_tensor(total[:, :], total[:, :], s[:, at], ALU.mult).then_inc(chain, 1)
                dve.wait_ge(chain, 2)
                nc.vector.tensor_tensor(x[:, at], x[:, at], total[:, :], ALU.add).then_inc(chain, 1)
                dve.wait_ge(chain, 3)

NCHUNKS = len(DCH)
MAX_BANKS = ((5, 6), (7, 4))


def shift_tokens(nc, name, x, out, also=None):
    with Stage(nc, name) as st:
        copied, loaded = st.sem("copied"), st.sem("loaded")
        half = C // 2
        xv = x[:, :].rearrange("p (b t) -> p b t", b=B)
        ov = out[:, :].rearrange("p (b t) -> p b t", b=B)
        with nc.Block() as block:

            @block.scalar
            def _(act):
                nc.scalar.activation(out[0:half, :], x[0:half, :], ACT.Copy).then_inc(copied, 1)
                act.wait_ge(copied, 1)

            @block.vector
            def _(dve):
                nc.vector.tensor_copy(ov[half:, :, 1:], xv[half:, :, :L - 1]).then_inc(loaded, 1)
                nc.vector.memset(ov[half:, :, 0:1], 0.0).then_inc(loaded, 1)
                dve.wait_ge(loaded, 2)


def load_layer(nc, layer, pairs, tables, scales):
    with Stage(nc, "layer") as st:
        loaded, scaled = st.sem("loaded"), st.sem("scaled")
        with nc.Block() as block:

            @block.sync
            def _(sp):
                for dst, src in pairs:
                    sp.dma_start(dst, src[bass.ds(layer, 1)].squeeze(0)).then_inc(loaded, 16)
                for dst, src in tables:
                    sp.dma_start(dst[:, :], src).then_inc(loaded, 16)
                sp.wait_ge(loaded, 16 * (len(pairs) + len(tables)))

            @block.vector
            def _(dve):
                dve.wait_ge(loaded, 16 * (len(pairs) + len(tables)))
                for n, (dst, _) in enumerate(tables):
                    nc.vector.tensor_scalar(dst[:, :], dst[:, :], scales[:, n:n + 1], None, ALU.mult).then_inc(scaled, 1)
                dve.wait_ge(scaled, len(tables))


def local_pair(nc, name, ps, k, now, after, w_dram, after_index, xs, tables, buf, cur):
    NQ = 2 * NCH
    qk, low, values = buf["qk"], buf["low"], buf["values"]
    square, part, sine = buf["square"], buf["part"], buf["sine"]
    prob, inverse, head_out = buf["prob"], buf["inverse"], buf["head_out"]
    with Stage(nc, name) as st:
        S = lambda *names: [st.sem(n) for n in names]
        fetched, projected, squared, bank_used, sined, added = S(
            "fetched", "projected", "squared", "bank_used", "sined", "added")
        norms, rooted, inverted, spread, normed, lowered = S("norms", "rooted", "inverted", "spread", "normed", "lowered")
        v_projected, v_out, max_scored, max_used, neg, rows, rows_out = S(
            "v_projected", "v_out", "max_scored", "max_used", "neg", "rows", "rows_out")
        scored, raised, weighed, recip, evened, mixed, done = S(
            "scored", "raised", "weighed", "recip", "evened", "mixed", "done")
        head = lambda h: slice(h * DH, (h + 1) * DH)
        last_of = lambda t: t % TILES == TILES - 1
        span = lambda t: P if last_of(t) else SPAN
        with nc.Block() as block:

            @block.sync
            def _(sp):
                sp.dma_start(after[:, :, :], w_dram[bass.ds(after_index, 1)].squeeze(0)).then_inc(fetched, 16)
                sp.wait_ge(fetched, 16)

            @block.tensor
            def _(pe):
                def norm(i):
                    pe.wait_ge(squared, i + 1)
                    q = i % 4 * QUAD
                    nc.tensor.matmul(ps[q:q + QUAD, 4, :], k["norm_row"][:, i // 4, :], square[:, i % 2, :],
                                     start=i < 4, stop=i >= NQ - 4).then_inc(norms, 1)

                for i in range(NQ):
                    c, n = divmod(i, 2)
                    if i >= 2:
                        pe.wait_ge(squared, i - 1)
                        pe.wait_ge(bank_used, i - 1)
                    for s in range(2):
                        last = nc.tensor.matmul(ps[:, 2 * n + s, :], now[:, 2 * n + s, :], xs[:, chunk(c)],
                                                start=True, stop=True)
                    last.then_inc(projected, 1)
                    if i:
                        norm(i - 1)
                norm(NQ - 1)
                for c in range(NCH):
                    if c >= 2:
                        pe.wait_ge(v_out, c - 1)
                    for t in range(4):
                        a = c * CH + t * P
                        last = nc.tensor.matmul(ps[:, 5 + c % 2, t * P:(t + 1) * P], xs[:, a:a + P], now[:, 4, :],
                                                start=True, stop=True)
                    last.then_inc(v_projected, 1)
                pe.wait_ge(inverted, 1)
                pe.wait_ge(bank_used, NQ)
                for i in range(NQ):
                    if i >= 4:
                        pe.wait_ge(normed, i - 3)
                    nc.tensor.matmul(ps[:, i % 4, :], k["norm_spread"][:, i, :], buf["norm"][:, :],
                                     start=True, stop=True).then_inc(spread, 1)
                pe.wait_ge(v_out, NCH)
                for g in range(B):
                    pe.wait_ge(lowered, 4 * (g + 1))
                    if g >= 2:
                        pe.wait_ge(max_used, 2 * (g - 1))
                    for h, bank in enumerate(MAX_BANKS[g % 2]):
                        nc.tensor.matmul(ps[:, bank, :], k["ident_b"][:, :], k["band_q"][:, :], start=True, stop=True)
                        for j in range(TILES):
                            for win in range(4):
                                at = g * L + j * P + win * WIN
                                back = 0 if j == 0 and win == 0 else WIN
                                last = nc.tensor.matmul(
                                    ps[win * WIN:(win + 1) * WIN, bank, j * 2 * WIN + WIN - back:(j + 1) * 2 * WIN],
                                    low[head(h), 0, at:at + WIN], low[head(h), 1, at - back:at + WIN],
                                    start=False, stop=True, skip_group_check=True)
                        last.then_inc(max_scored, 1)
                pe.wait_ge(neg, 4)
                nc.tensor.matmul(ps[:, 7, 0:P], buf["neg_parts"][:, :, :].rearrange("p s u -> p (s u)"),
                                 k["ident_b"][:, :], start=True, stop=True).then_inc(rows, 1)
                pe.wait_ge(rows_out, 1)

                def score(pair):
                    if pair >= 2:
                        pe.wait_ge(raised, pair - 1)
                    for h in range(2):
                        out = ps[:, pair % 2 * 2 + h, 0:2 * SPAN].rearrange("p (j n) -> p j n", j=2)
                        nc.tensor.matmul(out, k["ident_b"][:, :], k["band_k"][:, :].unsqueeze(1).to_broadcast([P, 2, SPAN]),
                                         start=True, stop=True)
                        for j in range(2):
                            t = 2 * pair + j
                            n, u = span(t), h * NT + t
                            nc.tensor.matmul(out[:, j, 0:P], k["unit_row"][:, u:u + 1].to_broadcast([P, P]),
                                             buf["rows"][:, :], start=False, stop=True, skip_group_check=True)
                            if n > P:
                                nc.tensor.matmul(out[:, j, P:n], k["unit_row"][:, u + 1:u + 2].to_broadcast([P, P]),
                                                 buf["rows"][:, 0:n - P], start=False, stop=True,
                                                 skip_group_check=True)
                            last = nc.tensor.matmul(out[:, j, 0:n], qk[head(h), 1, t * P:(t + 1) * P],
                                                    qk[head(h), 0, t * P:t * P + n], start=False, stop=True,
                                                    skip_group_check=True)
                    last.then_inc(scored, 1)

                def weigh(t):
                    c, j = divmod(t, 4)
                    pe.wait_ge(raised, t // 2 + 1)
                    if j == 0 and c >= 2:
                        pe.wait_ge(done, c - 1)
                    if j == 3 and c >= 1 and not last_of(t):
                        pe.wait_ge(done, c)
                    pieces = [(c, j * P, 0, min(span(t), CH - j * P))]
                    if pieces[0][3] < span(t):
                        pieces.append((c + 1, 0, P, span(t) - P))
                    for cc, to, frm, n in pieces:
                        opens = to == 0 and (j == 0 and c % 2 == 0 or cc > c)
                        for what, bank in ((None, 4), ("ones", 6)):
                            for h in range(2):
                                left = values[:, t, head(h)] if what is None else k["ones"][:, :]
                                last = nc.tensor.matmul(ps[head(h), bank + cc % 2, to:to + n], left,
                                                        prob[:, t // 2 % 2, h, t % 2, frm:frm + n], start=opens,
                                                        stop=True, skip_group_check=True)
                    last.then_inc(weighed, 1)

                def mix(c):
                    pe.wait_ge(evened, c + 1)
                    nc.tensor.matmul(ps[:, 6 + c % 2, :], now[:, 5, :], head_out[:, c % 2, :], start=True,
                                     stop=True).then_inc(mixed, 1)

                score(0)
                for t in range(NT):
                    if t % 2 == 0 and t + 2 < NT:
                        score(t // 2 + 1)
                    weigh(t)
                    if t >= 4 and t % 4 == 1:
                        mix(t // 4 - 1)
                mix(NCH - 1)

            @block.scalar
            def _(act):
                for i in range(NQ):
                    c, n = divmod(i, 2)
                    act.wait_ge(projected, i + 1)
                    if i >= 2:
                        act.wait_ge(norms, i - 1)
                    nc.scalar.activation(square[:, i % 2, :], ps[:, 2 * n, :], ACT.Square).then_inc(squared, 1)
                act.wait_ge(norms, NQ)
                nc.scalar.activation(buf["norm"][:, :], ps[:, 4, :], ACT.Sqrt).then_inc(rooted, 1)
                for c in range(NCH):
                    act.wait_ge(v_projected, c + 1)
                    nc.scalar.activation(values[:, 4 * c:4 * c + 4, :],
                                         ps[:, 5 + c % 2, :].rearrange("p (t n) -> p t n", n=P),
                                         ACT.Copy).then_inc(v_out, 1)
                for i in range(NQ):
                    c, n = divmod(i, 2)
                    act.wait_ge(normed, i + 1)
                    nc.scalar.activation(low[:, n, chunk(c)], qk[:, n, chunk(c)], ACT.Copy).then_inc(lowered, 1)
                for pair in range(NT // 2):
                    act.wait_ge(scored, pair + 1)
                    if pair >= 2:
                        act.wait_ge(weighed, 2 * (pair - 1))
                    bank = pair % 2 * 2
                    s = ps[:, bank:bank + 2, 0:2 * SPAN].rearrange("p h (j n) -> p h j n", j=2)
                    whole = not last_of(2 * pair + 1)
                    for js, n in [(slice(0, 2), SPAN)] if whole else [(0, SPAN), (1, P)]:
                        last = nc.scalar.activation(prob[:, pair % 2, :, js, 0:n], s[:, :, js, 0:n], ACT.Exp,
                                                    scale=QK_SCALE)
                    last.then_inc(raised, 1)

            @block.vector
            def _(dve):
                for i in range(NQ):
                    c, n = divmod(i, 2)
                    at = slice(c % 2 * CH, (c % 2 + 1) * CH)
                    dve.wait_ge(projected, i + 1)
                    if i >= 2:
                        dve.wait_ge(added, i - 1)
                    nc.vector.tensor_tensor(sine[:, i % 2, :], ps[:, 2 * n + 1, :], tables[2 * n + 1][:, at],
                                            ALU.mult).then_inc(sined, 1)
                    dve.wait_ge(squared, i + 1)
                    nc.vector.tensor_tensor(part[:, i % 2, :], ps[:, 2 * n, :], tables[2 * n][:, at],
                                            ALU.mult).then_inc(bank_used, 1)
                    dve.wait_ge(sined, i + 1)
                    dve.wait_ge(bank_used, i + 1)
                    nc.vector.tensor_tensor(qk[:, n, chunk(c)], part[:, i % 2, :], sine[:, i % 2, :],
                                            ALU.add).then_inc(added, 1)
                dve.wait_ge(rooted, 1)
                nc.vector.tensor_scalar(buf["norm"][:, :], buf["norm"][:, :], 1e-12, None, ALU.max).then_inc(rooted, 1)
                dve.wait_ge(rooted, 2)
                nc.vector.reciprocal(buf["norm"][:, :], buf["norm"][:, :]).then_inc(inverted, 1)
                dve.wait_ge(added, NQ)
                for i in range(NQ):
                    c, n = divmod(i, 2)
                    dve.wait_ge(spread, i + 1)
                    nc.vector.tensor_tensor(qk[:, n, chunk(c)], qk[:, n, chunk(c)], ps[:, i % 4, :],
                                            ALU.mult).then_inc(normed, 1)
                for g in range(B):
                    for h, bank in enumerate(MAX_BANKS[g % 2]):
                        dve.wait_ge(max_scored, 2 * g + h + 1)
                        nc.vector.reduce_max(buf["top"][:, h * NT + g * TILES:h * NT + (g + 1) * TILES],
                                             ps[:, bank, :].rearrange("p (u n) -> p u n", n=2 * WIN),
                                             AX_X).then_inc(max_used, 1)
                dve.wait_ge(max_used, 2 * B)
                link = Chain(dve, neg)
                top, parts = buf["top"], buf["neg_parts"]
                link(nc.vector.tensor_scalar(top[:, :], top[:, :], -1.0, None, ALU.mult))
                link(nc.vector.tensor_copy(parts[:, 0, :], top[:, :]))
                link(nc.vector.tensor_tensor(top[:, :], top[:, :], parts[:, 0, :], ALU.subtract))
                link(nc.vector.tensor_copy(parts[:, 1, :], top[:, :]))
                dve.wait_ge(rows, 1)
                nc.vector.tensor_copy(buf["rows"][:, :], ps[:, 7, 0:P]).then_inc(rows_out, 1)
                for c in range(NCH):
                    dve.wait_ge(weighed, 4 * c + 4)
                    if c:
                        dve.wait_ge(evened, c)
                    nc.vector.reciprocal(inverse[:, :], ps[:, 6 + c % 2, :]).then_inc(recip, 1)
                    dve.wait_ge(recip, c + 1)
                    nc.vector.tensor_tensor(head_out[:, c % 2, :], ps[:, 4 + c % 2, :], inverse[:, :],
                                            ALU.mult).then_inc(evened, 1)
                    dve.wait_ge(mixed, c + 1)
                    nc.vector.tensor_tensor(cur[:, chunk(c)], cur[:, chunk(c)], ps[:, 6 + c % 2, :],
                                            ALU.add).then_inc(done, 1)
                dve.wait_ge(done, NCH)


def gated_network(nc, ps, xn, w1, w2, b1, b2, cur):
    units = [(c, f) for c in range(NCH) for f in range(NCHUNKS)]
    with Stage(nc, "gn") as st:
        gate, product = st.sb("gate", [P, 2, CH]), st.sb("product", [P, 2, CH])
        lefts, gates, gelus, gated, summed, done = (st.sem(n) for n in ("lefts", "gates", "gelus", "gated", "summed", "done"))
        def finish(dve, c):
            dve.wait_ge(summed, NCHUNKS * (c + 1))
            nc.vector.scalar_tensor_tensor(out=cur[:, chunk(c)], in0=ps[:, 4 + c % 2, :], scalar=b2,
                                           in1=cur[:, chunk(c)], op0=ALU.add, op1=ALU.add).then_inc(done, 1)

        with nc.Block() as block:

            @block.tensor
            def _(pe):
                def down(u):
                    c, f = units[u]
                    m = DCH[f][1]
                    pe.wait_ge(gated, u + 1)
                    if f == 0 and c >= 2:
                        pe.wait_ge(done, c - 1)
                    nc.tensor.matmul(ps[:, 4 + c % 2, :], w2[0:m, f, :], product[0:m, u % 2, :], start=f == 0,
                                     stop=f == NCHUNKS - 1).then_inc(summed, 1)

                for u, (c, f) in enumerate(units):
                    o, m = DCH[f]
                    if u >= 2:
                        pe.wait_ge(gated, u - 1)
                    nc.tensor.matmul(ps[0:m, u % 2, :], w1[:, DI + o:DI + o + m], xn[:, chunk(c)],
                                     start=True, stop=True).then_inc(gates, 1)
                    nc.tensor.matmul(ps[0:m, 2 + u % 2, :], w1[:, o:o + m], xn[:, chunk(c)],
                                     start=True, stop=True).then_inc(lefts, 1)
                    if u:
                        down(u - 1)
                down(len(units) - 1)

            @block.scalar
            def _(act):
                for u, (c, f) in enumerate(units):
                    m = DCH[f][1]
                    act.wait_ge(gates, u + 1)
                    if u >= 2:
                        act.wait_ge(gated, u - 1)
                    nc.scalar.activation(gate[0:m, u % 2, :], ps[0:m, u % 2, :], ACT.Gelu,
                                         bias=b1[0:m, NCHUNKS + f:NCHUNKS + f + 1]).then_inc(gelus, 1)

            @block.vector
            def _(dve):
                for u, (c, f) in enumerate(units):
                    m = DCH[f][1]
                    dve.wait_ge(gelus, u + 1)
                    dve.wait_ge(lefts, u + 1)
                    if u >= 2:
                        dve.wait_ge(summed, u - 1)
                    nc.vector.scalar_tensor_tensor(out=product[0:m, u % 2, :], in0=ps[0:m, 2 + u % 2, :],
                                                   scalar=b1[0:m, f:f + 1], in1=gate[0:m, u % 2, :],
                                                   op0=ALU.add, op1=ALU.mult).then_inc(gated, 1)
                    if f == 1 and c:
                        finish(dve, c - 1)
                finish(dve, NCH - 1)
                dve.wait_ge(done, NCH)


def gate_and_store(nc, ps, x, s, g, out):
    with Stage(nc, "end") as st:
        silus, products, sums, stored = (st.sem(n) for n in ("silus", "products", "sums", "stored"))
        with nc.Block() as block:

            @block.scalar
            def _(act):
                for c in range(NCH):
                    nc.scalar.activation(g[:, chunk(c)], g[:, chunk(c)], ACT.Silu).then_inc(silus, 1)

            @block.vector
            def _(dve):
                for c in range(NCH):
                    dve.wait_ge(silus, c + 1)
                    nc.vector.tensor_tensor(s[:, chunk(c)], s[:, chunk(c)], g[:, chunk(c)], ALU.mult).then_inc(products, 1)
                    dve.wait_ge(products, c + 1)
                    nc.vector.tensor_tensor(x[:, chunk(c)], x[:, chunk(c)], s[:, chunk(c)], ALU.add).then_inc(sums, 1)

            @block.sync
            def _(sp):
                for c in range(NCH):
                    sp.wait_ge(sums, c + 1)
                    sp.dma_start(out[:, chunk(c)], x[:, chunk(c)]).then_inc(stored, 16)
                sp.wait_ge(stored, 16 * NCH)


def build_program(nc, a, out):
    with ExitStack() as whole:
        def buffers(ctx, names):
            return {n: ctx.enter_context(nc.sbuf_tensor("sb_" + n, list(a[n].shape), a[n].dtype)) for n in names}

        def loads(tensors):
            return [(t[:], a[n]) for n, t in tensors.items()]

        ps = whole.enter_context(nc.psum_tensor("ps", [P, 8, CH], F32))
        k = buffers(whole, CONSTANTS)
        x, s, cur = (whole.enter_context(nc.sbuf_tensor(n, [P, T], F32)) for n in ("x", "s", "cur"))
        q_parts, k_parts = (nc.dram_tensor(n, [3, C, T + L], BF16).ap() for n in ("q_parts", "k_parts"))

        with ExitStack() as ctx:
            w = buffers(ctx, [n for n in a if n.startswith("ta_") and n != "ta_bv"])
            w["ta_bv"] = ctx.enter_context(nc.sbuf_tensor("sb_ta_bv", [P, P], F32))
            load_constants(nc, loads(k) + [(x[:, :], a["x"])] +
                           [(t[:], a[n].to_broadcast([P, P]) if n == "ta_bv" else a[n]) for n, t in w.items()])
            layernorm(nc, "ln0", ps, k, x, cur)
            tile_attention(nc, ps, k, w, cur, s)

        with ExitStack() as ctx:
            vtok = ctx.enter_context(nc.sbuf_tensor("vtok0", [P, NT, P], F32))
            w = buffers(ctx, ["cq", "ck", "cv", "cqs", "cks", "cproj", "taps", "ln1"])
            with ExitStack() as inner:
                h, mixed = (inner.enter_context(nc.sbuf_tensor(n, [P, T], F32)) for n in ("h0", "h_mixed"))
                tables = buffers(inner, ["cos", "sin"])
                load_constants(nc, loads(w) + loads(tables))
                layernorm(nc, "ln1", ps, k, cur, h, w["ln1"][:, 0:1], w["ln1"][:, 1:2])
                causal_convolution(nc, w["taps"], h, mixed)
                causal_inputs(nc, "ci0", ps, mixed, dict(q=w["cq"], k=w["ck"], v=w["cv"], q_swapped=w["cqs"],
                                                         k_swapped=w["cks"]), tables, q_parts, k_parts, vtok)
            causal_attention(nc, "ca0", ps, k, q_parts, k_parts, vtok, w["cproj"], cur, cur)
        with ExitStack() as ctx:
            h = ctx.enter_context(nc.sbuf_tensor("h1", [P, T], F32))
            mask = ctx.enter_context(nc.sbuf_tensor("mask", [P, NT, E], BF16))
            w = buffers(ctx, ["wv", "wp", "router", "ln2"])
            load_constants(nc, loads(w))
            layernorm(nc, "ln2", ps, k, cur, h, w["ln2"][:, 0:1], w["ln2"][:, 1:2])
            route(nc, ps, w["router"], h, mask)
            experts(nc, ps, k, w["wv"], w["wp"], h, mask, cur, s, x)

        with ExitStack() as ctx:
            vtok = ctx.enter_context(nc.sbuf_tensor("vtok1", [P, NT, P], F32))
            w = buffers(ctx, ["dq", "dk", "dv", "dproj"])
            load_constants(nc, loads(w))
            layernorm(nc, "ln3", ps, k, x, cur)
            causal_inputs(nc, "ci1", ps, cur, dict(q=w["dq"], k=w["dk"], v=w["dv"]), None, q_parts, k_parts, vtok)
            causal_attention(nc, "ca1", ps, k, q_parts, k_parts, vtok, w["dproj"], s, None)

        with ExitStack() as ctx:
            sb = lambda n, shape, dt=F32: ctx.enter_context(nc.sbuf_tensor(n, shape, dt))
            xs = sb("shifted", [P, T])
            tables = [sb(f"table{n}", [P, L]) for n in range(4)]
            pair_w = [sb(f"pair_w{n}", [P, 6, P]) for n in range(2)]
            scales, w1, w2 = sb("scales", [P, 4]), sb("w1", [P, 2 * DI]), sb("w2", [P, NCHUNKS, C])
            b1, small = sb("b1", [P, 2 * NCHUNKS]), sb("small", [P, 3])
            load_constants(nc, [(pair_w[0][:], a["pair_w"][0])])
            with nc.Fori(0, LAYERS) as layer:
                load_layer(nc, layer, [(scales[:], a["scales"]), (w1[:], a["w1"]), (w2[:], a["w2"]), (b1[:], a["b1"]),
                                       (small[:], a["small"])], [(t, a[f"table{n}"]) for n, t in enumerate(tables)],
                           scales)
                shift_tokens(nc, "shift1", cur, xs)
                with ExitStack() as inner:
                    new = lambda n, shape, dt=F32: inner.enter_context(nc.sbuf_tensor("pair_" + n, shape, dt))
                    buf = dict(qk=new("qk", [P, 2, T]), low=new("low", [P, 2, T], BF16), values=new("values", [P, NT, P]),
                               square=new("square", [P, 2, CH]), part=new("part", [P, 2, CH]), sine=new("sine", [P, 2, CH]),
                               prob=new("prob", [P, 2, 2, 2, SPAN]), inverse=new("inverse", [P, CH]),
                               head_out=new("head_out", [P, 2, CH]), norm=new("norm", [P, CH]), top=new("top", [P, 2 * NT]),
                               neg_parts=new("neg_parts", [P, 2, 2 * NT], BF16), rows=new("rows", [P, P], BF16))
                    with nc.Fori(0, PAIRS // 2) as two:
                        for u in range(2):
                            local_pair(nc, f"pair{u}", ps, k, pair_w[u], pair_w[1 - u], a["pair_w"],
                                       layer * PAIRS + two * 2 + (u + 1), xs, tables, buf, cur)
                shift_tokens(nc, "shift2", cur, xs)
                with nc.sbuf_tensor("normed", [P, T], F32) as normed:
                    layernorm(nc, "ln4", ps, k, xs, normed, small[:, 0:1], small[:, 1:2])
                    gated_network(nc, ps, normed, w1, w2, b1, small[:, 2:3], cur)
        gate_and_store(nc, ps, x, s, cur, out)


CONSTANTS = ["ident", "ident_b", "mean", "mean_row", "pick_row", "after_q", "after_k", "pick_total", "spread_total",
             "norm_row", "norm_spread", "band_q", "band_k", "unit_row", "ones"]


def constants():
    f, bf = np.float32, mybir.dt.np(BF16)
    c = {"ident": np.eye(P, dtype=f), "ident_b": np.eye(P).astype(bf), "mean": np.full((P, P), 1.0 / C, f),
         "ones": np.ones((P, DH), f)}
    c["mean_row"], c["pick_row"] = np.zeros((P, 2, QUAD), f), np.zeros((P, NCH, P), f)
    for j in range(2):
        c["mean_row"][:, j, j] = 1.0 / C
    for i in range(NCH):
        c["pick_row"][i % 4 * QUAD + i // 4, i, :] = 1
    at = np.arange(P)
    c["after_q"] = np.where(at[None, :] > at[:, None], MASKED, 0).astype(bf)
    c["after_k"] = np.ascontiguousarray(c["after_q"].T)
    c["pick_total"], c["spread_total"] = np.zeros((P, 2 * GROUPS, QUAD), f), np.zeros((QUAD, 2 * GROUPS, P), f)
    for u in range(2 * GROUPS):
        for h in range(HG):
            c["pick_total"][h * QUAD + HD, u, HG * u + h] = 1
            c["spread_total"][HG * u + h, u, h * QUAD:(h + 1) * QUAD] = 1
    c["norm_row"], c["norm_spread"] = np.zeros((P, 4, QUAD), f), np.zeros((P, 2 * NCH, P), f)
    for h in range(2):
        for j in range(4):
            c["norm_row"][h * DH:(h + 1) * DH, j, 2 * j + h] = 1
        for i in range(2 * NCH):
            c["norm_spread"][i % 4 * QUAD + 2 * (i // 4) + h, i, h * DH:(h + 1) * DH] = 1
    q, key = at % WIN, np.arange(2 * WIN) - WIN
    seen = (key[None, :] <= q[:, None]) & (key[None, :] >= q[:, None] - WIN)
    band = np.tile(np.where(seen, 0, MASKED)[:, None, :], (1, TILES, 1))
    band[:WIN, 0, :WIN] = MASKED
    c["band_q"] = band.reshape(P, TILES * 2 * WIN).astype(bf)
    ahead = np.arange(SPAN)[None, :] - at[:, None]
    c["band_k"] = np.where((ahead >= 0) & (ahead <= WIN), 0, MASKED).astype(bf)
    c["unit_row"] = np.tile(np.eye(2 * NT), (2, 1)).astype(bf)
    inv = (1.0 / f(10000.0) ** (np.arange(0, HD, 2, dtype=f) / HD)).astype(f)
    angle = np.tile(np.arange(L, dtype=f)[None, :] * inv[:, None], (2, 1))
    sign = np.repeat(np.array([-1, 1], f), HD // 2)[:, None]
    c["cos"] = np.tile(np.cos(angle), (HEADS, 1)).astype(f)
    c["sin"] = np.tile(np.sin(angle) * sign, (HEADS, 1)).astype(f)
    half = np.arange(0, DH, 2, dtype=f)
    inv = (f(1.0) / f(10000.0) ** (half / f(DH))).astype(f)
    t = np.arange(L, dtype=f)
    angle = np.tile((t[:, None] * inv[None, :]).astype(f), (1, 2))
    base = ((half + f(0.4 * DH)) / f(1.4 * DH)).astype(f)
    power = ((t - L // 2) / f(WIN // 2)).astype(f)
    grow = np.tile((base[None, :] ** power[:, None]).astype(f), (1, 2))
    sign = np.repeat(np.array([-1, 1], f), DH // 2)
    for n, table in enumerate((np.cos(angle) * grow, np.sin(angle) * grow * sign,
                               np.cos(angle) * (f(1) / grow), np.sin(angle) * (f(1) / grow) * sign)):
        c[f"table{n}"] = np.ascontiguousarray(np.tile(table.astype(f).T, (2, 1)))
    return c


def lay_out(i):
    A = np.ascontiguousarray
    col = lambda v: A(v[:, None])

    def swapped(w, width):
        n = w.shape[-1]
        return A(w[..., np.arange(n).reshape(-1, 2, width // 2)[:, ::-1].reshape(-1)])

    def head_rows(w):
        o = np.zeros((P, GROUPS, C), w.dtype)
        for g in range(GROUPS):
            for h in range(HG):
                o[h * QUAD:h * QUAD + HD, g] = w[(g * HG + h) * HD:(g * HG + h + 1) * HD]
        return o

    d = {"x": A(i["L0_attn_batch"].reshape(T, C).T)}
    for n in "qkvo":
        d["ta_" + n] = A(i["L0_attn_W" + n].T)
        d["ta_b" + n] = i["L0_attn_b" + n][None, :] if n == "v" else col(i["L0_attn_b" + n])
    w = i["L0_ffn_attn_w"]
    d["cq"], d["ck"], d["cv"] = A(w[:, :C]), A(w[:, C:2 * C]), A(w[:, 2 * C:])
    d["cqs"], d["cks"] = swapped(d["cq"], HD), swapped(d["ck"], HD)
    d["cproj"] = head_rows(i["L0_ffn_proj_w"])
    d["taps"] = A(i["L0_ffn_conv_w"][:, 0, :])
    for n in (1, 2):
        d[f"ln{n}"] = A(np.stack([i[f"L0_ffn_ln{n}_w"], i[f"L0_ffn_ln{n}_b"]], 1))
    d["router"] = i["L0_ffn_router_w"]
    d["wv"] = A(i["L0_ffn_expert_wv"].transpose(1, 0, 2))
    d["wp"] = A(i["L0_ffn_expert_proj"].reshape(E, DFF // P, P, C).transpose(2, 0, 1, 3))
    w = i["L1_attn_w_qkv"].T
    d["dq"], d["dk"], d["dv"] = A(w[:, :C]), A(w[:, C:2 * C]), A(w[:, 2 * C:])
    d["dproj"] = head_rows(i["L1_attn_w_proj"].T)
    w = i["L1_ffn_Wqkv"]
    q, key, v = w[..., :INNER], w[..., INNER:2 * INNER], w[..., 2 * INNER:]
    pair = lambda m: m.reshape(LAYERS, C, PAIRS, P).transpose(0, 2, 1, 3)
    parts = [pair(q), pair(swapped(q, DH)), pair(key), pair(swapped(key, DH)), pair(v),
             i["L1_ffn_Wo"].reshape(LAYERS, PAIRS, P, C)]
    w = np.stack(parts, 3).reshape(LAYERS * PAIRS, P, 6, P)
    d["pair_w"] = A(np.concatenate([w, w[:1]]))
    cols = []
    for n in ("q", "k"):
        m = i[f"L1_ffn_{n}_scale"]
        for v in (m, np.concatenate([m[:, DH // 2:], m[:, :DH // 2]], 1)):
            cols.append(np.concatenate([v, v], 1))
    d["scales"] = A(np.stack(cols, 2))
    d["w1"] = i["L1_ffn_W1"]
    d["b1"], d["w2"] = np.zeros((LAYERS, P, 2 * NCHUNKS), np.float32), np.zeros((LAYERS, P, NCHUNKS, C), np.float32)
    for n, (o, m) in enumerate(DCH):
        d["b1"][:, :m, n] = i["L1_ffn_b1"][:, o:o + m]
        d["b1"][:, :m, NCHUNKS + n] = i["L1_ffn_b1"][:, DI + o:DI + o + m]
        d["w2"][:, :m, n] = i["L1_ffn_W2"][:, o:o + m]
    d["small"] = A(np.stack([i["L1_ffn_ln_g"], i["L1_ffn_ln_b"], i["L1_ffn_b2"]], 2))
    return d


def kernel(**inputs):
    import concourse.bacc as bacc
    from concourse.bass_utils import run_bass_kernel_spmd

    nc = bacc.Bacc("TRN2", target_bir_lowering=False, num_devices=1)
    host = {n: np.asarray(v) for n, v in inputs.items()}
    arrays, a = {}, {}
    for name, v in {**constants(), **lay_out(host)}.items():
        arrays["in_" + name] = np.ascontiguousarray(v)
        a[name] = nc.dram_tensor("in_" + name, v.shape, mybir.dt.from_np(v.dtype), kind="ExternalInput").ap()
    out = nc.dram_tensor("out", [C, T], F32, kind="ExternalOutput").ap()
    build_program(nc, a, out)
    result = run_bass_kernel_spmd(nc, [arrays], core_ids=[0])
    return np.ascontiguousarray(result.results[0]["out"].T).reshape(B, L, C)
```

```python
from contextlib import ExitStack

import numpy as np
import concourse.bass as bass
from concourse import mybir

ALU = mybir.AluOpType
ACT = mybir.ActivationFunctionType
AX_X = mybir.AxisListType.X
F32 = mybir.dt.float32
BF16 = mybir.dt.bfloat16

P = 128
C = 128
B = 4
L = 1024
T = B * L
CH = 512
NCH = T // CH
NT = T // P
TILES = L // P
QUAD = 32
EPS = 1e-5
MASKED = -1e30

HEADS = 16
HD = C // HEADS
HG = 4
GROUPS = HEADS // HG
PRODUCTS = ((0, 0), (0, 1), (0, 2), (1, 0), (1, 1), (2, 0))
STACK = len(PRODUCTS) * HD
SHIFT_ROW = 64
KROWS = SHIFT_ROW + 2

E = 4
DFF = 512

LAYERS = 6
DH = 64
INNER = HEADS * DH
PAIRS = HEADS // 2
WIN = 32
SPAN = P + WIN
DI = int(C * 4 * 2 / 3)
DCH = [(o, min(P, DI - o)) for o in range(0, DI, P)]
SEEN = DH + WIN
QK_SCALE = 8.0

FIRST_SEM = 150


class Stage:

    def __init__(self, nc, name):
        self.nc, self.name, self.ctx, self.sems = nc, name, ExitStack(), []

    def __enter__(self):
        return self

    def __exit__(self, kind, *rest):
        if kind is None and self.sems:
            self.nc.all_engine_barrier(sems_to_clear=range(FIRST_SEM, FIRST_SEM + len(self.sems)))
        self.ctx.close()
        return False

    def sem(self, name):
        number = FIRST_SEM + len(self.sems)
        self.sems.append(self.ctx.enter_context(self.nc.semaphore(f"{self.name}_{name}", num=number)))
        return self.sems[-1]

    def sb(self, name, shape, dt=F32):
        return self.ctx.enter_context(self.nc.sbuf_tensor(f"{name}_of_{self.name}", shape, dt))


class Chain:

    def __init__(self, eng, sem, n=0):
        self.eng, self.sem, self.n = eng, sem, n

    def __call__(self, ins):
        self.n += 1
        ins.then_inc(self.sem, 1)
        self.eng.wait_ge(self.sem, self.n)


def in_parts(nc, k, cut, value, parts):
    cut(nc.vector.tensor_copy(parts, value))
    cut(nc.vector.scalar_tensor_tensor(out=value, in0=parts, scalar=k["minus_first"][:, 0:1], in1=value, op0=ALU.mult,
                                       op1=ALU.add))
    cut(nc.vector.tensor_copy(parts, value))
    return nc.vector.scalar_tensor_tensor(out=parts, in0=parts, scalar=k["minus_second"][:, 0:1], in1=value,
                                          op0=ALU.mult, op1=ALU.add)


def chunk(c):
    return slice(c * CH, (c + 1) * CH)


def load_constants(nc, pairs):
    with Stage(nc, "load") as st:
        loaded = st.sem("loaded")
        with nc.Block() as block:

            @block.sync
            def _(sp):
                for dst, src in pairs:
                    sp.dma_start(dst, src).then_inc(loaded, 16)
                sp.wait_ge(loaded, 16 * len(pairs))


def layernorm(nc, name, ps, k, src, dst, weight=None, bias=None):
    with Stage(nc, name) as st:
        square = st.sb("square", [P, 4, CH])
        rstd = st.sb("rstd", [P, CH])
        mean_ready, centred, squared = st.sem("mean_ready"), st.sem("centred"), st.sem("squared")
        var_part, var_eps, rooted = st.sem("var_part"), st.sem("var_eps"), st.sem("rooted")
        inverse, spread, scaled, done = st.sem("inverse"), st.sem("spread"), st.sem("scaled"), st.sem("done")
        with nc.Block() as block:

            @block.tensor
            def _(pe):
                for c in range(NCH):
                    if c >= 4:
                        pe.wait_ge(centred, c - 3)
                    nc.tensor.matmul(ps[:, c % 4, :], k["mean"][:, :], src[:, chunk(c)],
                                     start=True, stop=True).then_inc(mean_ready, 1)
                for c in range(NCH):
                    pe.wait_ge(squared, c + 1)
                    q = c % 4 * QUAD
                    nc.tensor.matmul(ps[q:q + QUAD, 4, :], k["mean_row"][:, c // 4, :], square[:, c % 4, :],
                                     start=c < 4, stop=c >= 4).then_inc(var_part, 1)
                pe.wait_ge(inverse, 1)
                for c in range(NCH):
                    if c >= 4:
                        pe.wait_ge(scaled, c - 3)
                    nc.tensor.matmul(ps[:, c % 4, :], k["pick_row"][:, c, :], rstd[:, :],
                                     start=True, stop=True).then_inc(spread, 1)

            @block.scalar
            def _(act):
                for c in range(NCH):
                    act.wait_ge(centred, c + 1)
                    if c >= 4:
                        act.wait_ge(var_part, c - 3)
                    nc.scalar.activation(square[:, c % 4, :], dst[:, chunk(c)], ACT.Square).then_inc(squared, 1)
                act.wait_ge(var_eps, 1)
                nc.scalar.activation(rstd[:, :], rstd[:, :], ACT.Sqrt).then_inc(rooted, 1)
                if weight is not None:
                    for c in range(NCH):
                        act.wait_ge(scaled, c + 1)
                        nc.scalar.activation(dst[:, chunk(c)], dst[:, chunk(c)], ACT.Identity,
                                             bias=bias, scale=weight).then_inc(done, 1)
                    act.wait_ge(done, NCH)

            @block.vector
            def _(dve):
                for c in range(NCH):
                    dve.wait_ge(mean_ready, c + 1)
                    nc.vector.tensor_tensor(dst[:, chunk(c)], src[:, chunk(c)], ps[:, c % 4, :],
                                            ALU.subtract).then_inc(centred, 1)
                dve.wait_ge(var_part, NCH)
                nc.vector.tensor_scalar(rstd[:, :], ps[:, 4, :], EPS, None, ALU.add).then_inc(var_eps, 1)
                dve.wait_ge(rooted, 1)
                nc.vector.reciprocal(rstd[:, :], rstd[:, :]).then_inc(inverse, 1)
                for c in range(NCH):
                    dve.wait_ge(spread, c + 1)
                    if c == 0:
                        dve.wait_ge(squared, NCH)
                    nc.vector.tensor_tensor(dst[:, chunk(c)], dst[:, chunk(c)], ps[:, c % 4, :],
                                            ALU.mult).then_inc(scaled, 1)
                dve.wait_ge(scaled, NCH)


def tile_attention(nc, ps, k, w, xn, out):
    scale = float(1.0 / np.sqrt(C))
    with nc.Fori(0, B) as b, Stage(nc, "ta") as st:
        x = st.sb("x", [P, L])
        qT = st.sb("qT", [P, L])
        kT = st.sb("kT", [P, L])
        v = st.sb("v", [P, TILES, P])
        prob = st.sb("prob", [P, 2, TILES, P])
        probT = st.sb("probT", [P, 2, TILES, P])
        outT = st.sb("outT", [P, 2, CH])
        top = st.sb("top", [P, TILES])
        total = st.sb("total", [P, 2, TILES])
        norm = st.sb("norm", [P, 1])
        got_x, projected, biased, v_ready = st.sem("got_x"), st.sem("projected"), st.sem("biased"), st.sem("v_ready")
        scored, shifted, raised, weighed = st.sem("scored"), st.sem("shifted"), st.sem("raised"), st.sem("weighed")
        turned, turned_out, summed, evened = st.sem("turned"), st.sem("turned_out"), st.sem("summed"), st.sem("evened")
        mixed, written, chain = st.sem("mixed"), st.sem("written"), st.sem("chain")
        with nc.Block() as block:

            @block.tensor
            def _(pe):
                pe.wait_ge(got_x, 1)
                for h in range(2):
                    for n, name in enumerate(("ta_q", "ta_k")):
                        nc.tensor.matmul(ps[:, 2 * n + h, :], w[name][:, :], x[:, chunk(h)],
                                         start=True, stop=True).then_inc(projected, 1)
                for t in range(TILES):
                    nc.tensor.matmul(ps[:, 4 + t // 4, t % 4 * P:(t % 4 + 1) * P], x[:, t * P:(t + 1) * P],
                                     w["ta_v"][:, :], start=True, stop=True).then_inc(projected, 1)
                pe.wait_ge(biased, 4)

                def score(t):
                    if t >= 2:
                        pe.wait_ge(shifted, t - 1)
                    for h in range(2):
                        last = nc.tensor.matmul(ps[:, t % 2 * 2 + h, :], qT[:, t * P:(t + 1) * P], kT[:, chunk(h)],
                                                start=True, stop=True)
                    last.then_inc(scored, 1)

                def turn(t):
                    pe.wait_ge(weighed, t + 1)
                    if t >= 1:
                        pe.wait_ge(turned_out, t)
                    else:
                        pe.wait_ge(v_ready, 2)
                    for j in range(TILES):
                        last = nc.tensor.transpose(ps[:, 4 + j // 4, j % 4 * P:(j % 4 + 1) * P],
                                                   prob[:, t % 2, j, :], k["ident"][:, :])
                    last.then_inc(turned, 1)

                def gather(t):
                    pe.wait_ge(turned_out, t + 1)
                    if t == 4:
                        pe.wait_ge(evened, 1)
                    for j in range(TILES):
                        last = nc.tensor.matmul(ps[:, 6, t % 4 * P:(t % 4 + 1) * P], v[:, j, :],
                                                probT[:, t % 2, j, :], start=j == 0, stop=j == TILES - 1)
                    last.then_inc(summed, 1)

                def mix(h):
                    pe.wait_ge(evened, h + 1)
                    if h:
                        pe.wait_ge(written, 1)
                    nc.tensor.matmul(ps[:, 7, :], w["ta_o"][:, :], outT[:, h, :], start=True,
                                     stop=True).then_inc(mixed, 1)

                score(0)
                score(1)
                for t in range(TILES):
                    if t + 2 < TILES:
                        score(t + 2)
                    if t:
                        gather(t - 1)
                    turn(t)
                    if t == 5:
                        mix(0)
                gather(TILES - 1)
                mix(1)

            @block.scalar
            def _(act):
                for h in range(2):
                    for n, (dst, bias) in enumerate(((qT, "ta_bq"), (kT, "ta_bk"))):
                        act.wait_ge(projected, 2 * h + n + 1)
                        nc.scalar.activation(dst[:, chunk(h)], ps[:, 2 * n + h, :], ACT.Identity,
                                             bias=w[bias][:, :]).then_inc(biased, 1)

                def copy_out(t):
                    act.wait_ge(turned, t + 1)
                    if t >= 2:
                        act.wait_ge(summed, t - 1)
                    nc.scalar.activation(probT[:, t % 2].rearrange("p j q -> p (j q)"),
                                         ps[:, 4:6, :].rearrange("p a n -> p (a n)"), ACT.Copy).then_inc(turned_out, 1)

                def finish(h):
                    act.wait_ge(mixed, h + 1)
                    nc.scalar.activation(out[:, bass.ds(b * L + h * CH, CH)], ps[:, 7, :], ACT.Identity,
                                         bias=w["ta_bo"][:, :]).then_inc(written, 1)

                for t in range(TILES):
                    act.wait_ge(shifted, t + 1)
                    nc.scalar.activation(prob[:, t % 2], prob[:, t % 2], ACT.Exp, scale=scale).then_inc(raised, 1)
                    if t >= 1:
                        copy_out(t - 1)
                    if t == 7:
                        finish(0)
                copy_out(TILES - 1)
                finish(1)
                act.wait_ge(written, 2)

            @block.vector
            def _(dve):
                link = Chain(dve, chain)
                nc.vector.tensor_copy(x[:, :], xn[:, bass.ds(b * L, L)]).then_inc(got_x, 1)
                dve.wait_ge(projected, 12)
                for a in range(2):
                    nc.vector.tensor_tensor(v[:, 4 * a:4 * a + 4, :], ps[:, 4 + a, :].rearrange("p (t n) -> p t n", n=P),
                                            w["ta_bv"][:, :].unsqueeze(1).to_broadcast([P, 4, P]),
                                            ALU.add).then_inc(v_ready, 1)

                def shift(t):
                    s = ps[:, t % 2 * 2:t % 2 * 2 + 2, :].rearrange("p a (j n) -> p (a j) n", n=P)
                    dve.wait_ge(scored, t + 1)
                    if t >= 1:
                        dve.wait_ge(shifted, t)
                    link(nc.vector.reduce_max(top[:, :], s, AX_X))
                    if t >= 2:
                        dve.wait_ge(turned, t - 1)
                    nc.vector.tensor_tensor(prob[:, t % 2], s, top[:, :].unsqueeze(2).to_broadcast([P, TILES, P]),
                                            ALU.subtract).then_inc(shifted, 1)

                def weigh(t):
                    a, r = total[:, 0, :], total[:, 1, :]
                    dve.wait_ge(raised, t + 1)
                    if t >= 1:
                        dve.wait_ge(weighed, t)
                    link(nc.vector.reduce_sum(a, prob[:, t % 2], AX_X))
                    link(nc.vector.reciprocal(r, a))
                    link(nc.vector.tensor_tensor(a, a, r, ALU.mult))
                    link(nc.vector.reduce_sum(norm[:, :], a, AX_X))
                    link(nc.vector.tensor_scalar(norm[:, :], norm[:, :], 1e-6, None, ALU.add))
                    link(nc.vector.reciprocal(norm[:, :], norm[:, :]))
                    link(nc.vector.tensor_scalar(r, r, norm[:, :], None, ALU.mult))
                    nc.vector.tensor_tensor(prob[:, t % 2], prob[:, t % 2],
                                            r.unsqueeze(2).to_broadcast([P, TILES, P]), ALU.mult).then_inc(weighed, 1)

                def even(h):
                    dve.wait_ge(summed, 4 * h + 4)
                    nc.vector.tensor_copy(outT[:, h, :], ps[:, 6, :]).then_inc(evened, 1)

                shift(0)
                for t in range(TILES):
                    if t + 1 < TILES:
                        shift(t + 1)
                    if t == 5:
                        even(0)
                    weigh(t)
                even(1)
                dve.wait_ge(evened, 2)


def causal_convolution(nc, taps, h, out):
    with Stage(nc, "conv") as st:
        chain = st.sem("chain")
        hv = h[:, :].rearrange("p (b t) -> p b t", b=B)
        ov = out[:, :].rearrange("p (b t) -> p b t", b=B)
        with nc.Block() as block:

            @block.vector
            def _(dve):
                link = Chain(dve, chain)
                link(nc.vector.tensor_scalar(ov, hv, taps[:, 2:3], None, ALU.mult))
                for back in (1, 2):
                    link(nc.vector.scalar_tensor_tensor(out=ov[:, :, back:], in0=hv[:, :, :L - back],
                                                        scalar=taps[:, 2 - back:3 - back], in1=ov[:, :, back:],
                                                        op0=ALU.mult, op1=ALU.add))


def causal_inputs(nc, name, ps, h, weights, tables, q_parts, k_parts, vtok):
    rotated = tables is not None
    with Stage(nc, name) as st:
        value = st.sb("value", [P, 2, CH])
        sine = st.sb("sine", [P, 2, CH])
        rest = st.sb("rest", [P, 2, CH])
        parts = st.sb("parts", [P, 4, 3, CH], BF16)
        projected, v_projected, bank_used = st.sem("projected"), st.sem("v_projected"), st.sem("bank_used")
        valued, high, rested, middle, low = (st.sem(n) for n in ("valued", "high", "rested", "middle", "low"))
        stored, v_out, chain = [st.sem(f"stored{n}") for n in range(4)], st.sem("v_out"), st.sem("chain")
        again = st.sem("again")
        with nc.Block() as block:

            @block.tensor
            def _(pe):
                for c in range(NCH):
                    for n in range(2):
                        i = 2 * c + n
                        if c:
                            pe.wait_ge(bank_used, i - 1)
                        last = nc.tensor.matmul(ps[:, 2 * n, :], weights["qk"[n]][:, :], h[:, chunk(c)],
                                                start=True, stop=True)
                        if rotated:
                            last = nc.tensor.matmul(ps[:, 2 * n + 1, :], weights["qk"[n] + "_swapped"][:, :],
                                                    h[:, chunk(c)], start=True, stop=True)
                        last.then_inc(projected, 1)
                    if c >= 2:
                        pe.wait_ge(v_out, c - 1)
                    for t in range(4):
                        a = c * CH + t * P
                        last = nc.tensor.matmul(ps[:, 4 + c % 2, t * P:(t + 1) * P], h[:, a:a + P], weights["v"][:, :],
                                                start=True, stop=True)
                    last.then_inc(v_projected, 1)

            @block.vector
            def _(dve):
                for c in range(NCH):
                    for n in range(2):
                        i, slot = 2 * c + n, c % 2 * 2 + n
                        dve.wait_ge(projected, i + 1)
                        if i >= 2:
                            dve.wait_ge(high, i - 1)
                            dve.wait_ge(rested, i - 1)
                        if rotated:
                            at = slice(c % 2 * CH, (c % 2 + 1) * CH)
                            nc.vector.tensor_tensor(value[:, n, :], ps[:, 2 * n, :], tables["cos"][:, at],
                                                    ALU.mult).then_inc(chain, 1)
                            if i >= 2:
                                dve.wait_ge(valued, i - 1)
                            nc.vector.tensor_tensor(sine[:, n, :], ps[:, 2 * n + 1, :], tables["sin"][:, at],
                                                    ALU.mult).then_inc(bank_used, 1)
                            dve.wait_ge(bank_used, i + 1)
                            dve.wait_ge(chain, i + 1)
                            nc.vector.tensor_tensor(value[:, n, :], value[:, n, :], sine[:, n, :],
                                                    ALU.add).then_inc(valued, 1)
                        else:
                            nc.vector.tensor_copy(value[:, n, :], ps[:, 2 * n, :]).then_inc(valued, 1)
                            dve.wait_ge(valued, i + 1)
                            dve.sem_inc(bank_used, 1)
                        dve.wait_ge(valued, i + 1)
                        dve.wait_ge(high, i + 1)
                        if i >= 2:
                            dve.wait_ge(low, i - 1)
                            dve.wait_ge(middle, i - 1)
                        nc.vector.tensor_tensor(rest[:, n, :], value[:, n, :], parts[:, slot, 0, :],
                                                ALU.subtract).then_inc(rested, 1)
                        dve.wait_ge(middle, i + 1)
                        nc.vector.tensor_tensor(parts[:, slot, 2, :], rest[:, n, :], parts[:, slot, 1, :],
                                                ALU.subtract).then_inc(low, 1)
                dve.wait_ge(low, 2 * NCH)

            @block.scalar
            def _(act):
                for c in range(NCH):
                    for n in range(2):
                        i, slot = 2 * c + n, c % 2 * 2 + n
                        act.wait_ge(valued, i + 1)
                        if c >= 2:
                            act.wait_ge(stored[slot], 16 * (c // 2))
                            act.wait_ge(again, 16 * min(2 * (c - 2) + n + 1, 2 * L // CH))
                        nc.scalar.activation(parts[:, slot, 0, :], value[:, n, :], ACT.Copy).then_inc(high, 1)
                        act.wait_ge(rested, i + 1)
                        nc.scalar.activation(parts[:, slot, 1, :], rest[:, n, :], ACT.Copy).then_inc(middle, 1)
                    act.wait_ge(v_projected, c + 1)
                    nc.scalar.activation(vtok[:, 4 * c:4 * c + 4, :], ps[:, 4 + c % 2, :].rearrange("p (t n) -> p t n", n=P),
                                         ACT.Copy).then_inc(v_out, 1)
                act.wait_ge(v_out, NCH)

            @block.sync
            def _(sp):
                for c in range(NCH):
                    for n, dram in enumerate((q_parts, k_parts)):
                        slot = c % 2 * 2 + n
                        sp.wait_ge(low, 2 * c + n + 1)
                        sp.dma_start(dram[:, :, chunk(c)].rearrange("s p t -> p s t"),
                                     parts[:, slot]).then_inc(stored[slot], 16)
                        if c < L // CH:
                            sp.dma_start(dram[:, :, chunk(NCH + c)].rearrange("s p t -> p s t"),
                                         parts[:, slot]).then_inc(again, 16)
                            sp.wait_ge(again, 16 * (2 * c + n + 1))
                for slot in range(4):
                    sp.wait_ge(stored[slot], 16 * (NCH // 2))


UNITS = [(qc, kt, max(0, kt - qc * 4) * P) for qc in range(2) for kt in range(4 * qc + 4)]
PIECES = [(h, qt, lo, min(CH, (qt + 1) * P - lo)) for h in range(HG) for qt in range(TILES)
          for lo in range(0, (qt + 1) * P, CH)]
PER_HEAD = len(PIECES) // HG


UNIT_PIECES = (3, 3, 2, 2, 5, 5, 5, 5, 6, 0, 6, 6)
ROWS_AFTER = 8
LEFT = sum(UNIT_PIECES[:ROWS_AFTER + 1])
AHEAD = len(PIECES) - LEFT
assert sum(UNIT_PIECES) == len(PIECES)


class Maxima:

    def __init__(self, nc, st, ps, k, buf):
        self.nc, self.ps, self.k, self.buf = nc, ps, k, buf
        self.scored, self.used, self.neg = st.sem("max_scored"), st.sem("max_used"), st.sem("max_neg")
        self.rows, self.rows_out, self.placed = st.sem("max_rows"), st.sem("max_rows_out"), st.sem("max_placed")

    def pe_piece(self, pe, step, stack, i):
        nc, ps, (queries, keys) = self.nc, self.ps, stack
        h, qt, lo, width = PIECES[i]
        bank, diagonal = 5 + step % 3, lo + width == (qt + 1) * P
        if step >= 3:
            pe.wait_ge(self.used, step - 2)
        last = nc.tensor.matmul(ps[:, bank, 0:width], queries[0:STACK, h, qt * P:(qt + 1) * P],
                                keys[0:STACK, h, lo:lo + width], start=True, stop=not diagonal)
        if diagonal:
            last = nc.tensor.matmul(ps[:, bank, width - P:width], self.k["ident_b"][:, :], self.k["after_q"][:, :],
                                    start=False, stop=True)
        last.then_inc(self.scored, 1)

    def pe_rows(self, pe, n):
        nc, ps = self.nc, self.ps
        pe.wait_ge(self.neg, 6 * (n + 1))
        for qt in range(TILES):
            last = nc.tensor.matmul(ps[0:2 * HG, 5 + qt // 4, qt % 4 * P:(qt % 4 + 1) * P],
                                    self.buf["neg_parts"][:, qt].rearrange("p h s -> p (h s)"), self.k["ident_b"][:, :],
                                    start=True, stop=True)
        last.then_inc(self.rows, 1)

    def dve_piece(self, dve, step, i):
        h, qt, lo, width = PIECES[i]
        dve.wait_ge(self.scored, step + 1)
        self.nc.vector.reduce_max(self.buf["top"][:, h, i % PER_HEAD:i % PER_HEAD + 1], self.ps[:, 5 + step % 3, 0:width],
                                  AX_X).then_inc(self.used, 1)

    def dve_rows(self, dve, n, steps):
        nc, top, neg, parts = self.nc, self.buf["top"], self.buf["neg"], self.buf["neg_parts"]
        dve.wait_ge(self.used, steps)
        link = Chain(dve, self.neg, 6 * n)
        half = TILES // 2
        late = top[:, :, half:].rearrange("p h (t s) -> p h t s", s=2)
        link(nc.vector.tensor_tensor(neg[:, :, half:], late[:, :, :, 0], late[:, :, :, 1], ALU.max))
        link(nc.vector.tensor_scalar(neg[:, :, half:], neg[:, :, half:], -1.0, None, ALU.mult))
        link(nc.vector.tensor_scalar(neg[:, :, :half], top[:, :, :half], -1.0, None, ALU.mult))
        turned = neg[:, :, :].rearrange("p h t -> p t h")
        link(nc.vector.tensor_copy(parts[:, :, :, 0], turned))
        link(nc.vector.tensor_tensor(turned, turned, parts[:, :, :, 0], ALU.subtract))
        link(nc.vector.tensor_copy(parts[:, :, :, 1], turned))
        dve.wait_ge(self.rows, n + 1)
        if n:
            dve.wait_ge(self.placed, 16 * HG * n)
        nc.vector.tensor_copy(self.buf["rows"][:, :], self.ps[0:2 * HG, 5:7, :].rearrange("p a n -> p (a n)"))\
            .then_inc(self.rows_out, 1)

    def sp_rows(self, sp, n, stack):
        sp.wait_ge(self.rows_out, n + 1)
        for h in range(HG):
            sp.dma_start(stack[0][SHIFT_ROW:SHIFT_ROW + 2, h, :], self.buf["rows"][2 * h:2 * h + 2, :])\
                .then_inc(self.placed, 16)


def load_stack(sp, sem, stack, q_parts, k_parts, first, group):
    for side, (dst, dram) in enumerate(zip(stack, (q_parts, k_parts))):
        for r, pair in enumerate(PRODUCTS):
            src = dram[pair[side], group * HG * HD:(group + 1) * HG * HD, bass.ds(first, L)]
            sp.dma_start(dst[r * HD:(r + 1) * HD, :, :], src.rearrange("(h d) t -> d h t", d=HD)).then_inc(sem, 16)
    return 16 * 2 * len(PRODUCTS)


def causal_attention(nc, name, ps, k, q_parts, k_parts, vtok, proj, out, residual):
    scale = float(1.0 / np.sqrt(HD))
    with ExitStack() as ctx:
        sb = lambda n, shape, dt=F32: ctx.enter_context(nc.sbuf_tensor(f"{n}_of_{name}", shape, dt))
        stacks = [(sb(f"queries{s}", [P, HG, L], BF16), sb(f"keys{s}", [P, HG, L], BF16)) for s in range(GROUPS)]
        prob = sb("prob", [P, 2, HG, CH])
        values = sb("values", [P, 2, TILES, HG, QUAD])
        summed = sb("summed", [P, 2, GROUPS, CH])
        inverse, inverse_parts = sb("inverse", [P, CH]), sb("inverse_parts", [P, CH], BF16)
        evened = sb("evened", [P, 2, CH])
        buf = dict(top=sb("top", [P, HG, PER_HEAD]), neg=sb("neg", [P, HG, TILES]),
                   neg_parts=sb("neg_parts", [P, TILES, HG, 2], BF16), rows=sb("rows", [2 * HG, L], BF16))

        with Stage(nc, name + "_first") as st:
            cleared, loaded = st.sem("cleared"), st.sem("loaded")
            maxima = Maxima(nc, st, ps, k, buf)
            with nc.Block() as block:

                @block.sync
                def _(sp):
                    for g in range(2):
                        sp.wait_ge(cleared, 3 * (g + 1))
                        n = load_stack(sp, loaded, stacks[g], q_parts, k_parts, 0, g)
                    sp.wait_ge(loaded, 2 * n)
                    maxima.sp_rows(sp, 0, stacks[0])
                    sp.wait_ge(maxima.placed, 16 * HG)

                @block.tensor
                def _(pe):
                    pe.wait_ge(loaded, 2 * 16 * 2 * len(PRODUCTS))
                    for i in range(len(PIECES)):
                        maxima.pe_piece(pe, i, stacks[0], i)
                    maxima.pe_rows(pe, 0)
                    pe.wait_ge(maxima.rows_out, 1)
                    for i in range(AHEAD):
                        maxima.pe_piece(pe, len(PIECES) + i, stacks[1], i)

                @block.vector
                def _(dve):
                    link = Chain(dve, cleared)
                    for q, kk in stacks:
                        link(nc.vector.memset(q[QUAD:SHIFT_ROW, :, :], 0.0))
                        link(nc.vector.memset(kk[QUAD:SHIFT_ROW, :, :], 0.0))
                        link(nc.vector.memset(kk[SHIFT_ROW:SHIFT_ROW + 2, :, :], 1.0))
                    link(nc.vector.memset(values[:, :, :, :, HD:], 0.0))
                    link(nc.vector.memset(values[:, :, :, :, HD:HD + 1], 1.0))
                    for i in range(len(PIECES)):
                        maxima.dve_piece(dve, i, i)
                    maxima.dve_rows(dve, 0, len(PIECES))
                    for i in range(AHEAD):
                        maxima.dve_piece(dve, len(PIECES) + i, i)
                    dve.wait_ge(maxima.used, len(PIECES) + AHEAD)

        with nc.Fori(0, B) as b, Stage(nc, name) as st:
            placed, loaded = st.sem("placed"), st.sem("loaded")
            scored, raised, weighed, acc_out = (st.sem(n) for n in ("scored", "raised", "weighed", "acc_out"))
            totals, parted, inverted, spread, even, projected, done = (
                st.sem(n) for n in ("totals", "parted", "inverted", "spread", "even", "projected", "done"))
            maxima = Maxima(nc, st, ps, k, buf)
            NU = len(UNITS)
            finals = [(half, g) for half in range(2) for g in range(GROUPS)]
            with nc.Block() as block:

                @block.sync
                def _(sp):
                    for g in range(GROUPS):
                        if g >= 2:
                            sp.wait_ge(scored, 2 * NU * (g - 1))
                        ahead = g + 2
                        n = load_stack(sp, loaded, stacks[ahead % GROUPS], q_parts, k_parts,
                                       (b + ahead // GROUPS) * L, ahead % GROUPS)
                        maxima.sp_rows(sp, g, stacks[(g + 1) % GROUPS])
                        sp.wait_ge(loaded, (g + 1) * n)
                    sp.wait_ge(maxima.placed, GROUPS * 16 * HG)

                @block.gpsimd
                def _(pool):
                    for g in range(GROUPS):
                        if g >= 2:
                            pool.wait_ge(weighed, NU * (g - 1))
                        src = vtok[:, bass.ds(b * TILES, TILES), g * HG * HD:(g + 1) * HG * HD]
                        nc.gpsimd.tensor_copy(values[:, g % 2, :, :, 0:HD], src.rearrange("p t (h d) -> p t h d", d=HD))\
                            .then_inc(placed, 1)
                        pool.wait_ge(placed, g + 1)

                @block.tensor
                def _(pe):
                    def pieces(g, count):
                        for _ in range(count):
                            n = next(step)
                            late = n % len(PIECES) >= LEFT
                            if n % len(PIECES) == LEFT:
                                pe.wait_ge(loaded, 16 * 2 * len(PRODUCTS) * (g + 1))
                                pe.wait_ge(maxima.rows_out, g + 1)
                            maxima.pe_piece(pe, n, stacks[(g + 1 + late) % GROUPS], (n + AHEAD) % len(PIECES))

                    def score(g, i, between=0):
                        qc, kt, j = UNITS[i]
                        queries, keys = stacks[g]
                        diagonal, u = kt >= 4 * qc, g * NU + i
                        if g and i == 0:
                            pe.wait_ge(maxima.placed, 16 * HG * g)
                        for pair in range(2):
                            if u:
                                pe.wait_ge(raised, 2 * u - 1 + pair)
                            for h in (2 * pair, 2 * pair + 1):
                                last = nc.tensor.matmul(ps[:, h, j:], keys[0:KROWS, h, kt * P:(kt + 1) * P],
                                                        queries[0:KROWS, h, qc * CH + j:(qc + 1) * CH],
                                                        start=True, stop=not diagonal)
                                if diagonal:
                                    last = nc.tensor.matmul(ps[:, h, j:j + P], k["ident_b"][:, :],
                                                            k["after_k"][:, :], start=False, stop=True)
                            last.then_inc(scored, 1)
                            pieces(g, between)

                    def weigh(g, i):
                        qc, kt, j = UNITS[i]
                        pe.wait_ge(raised, 2 * (g * NU + i) + 2)
                        if i == 0:
                            pe.wait_ge(placed, g + 1)
                        if kt == 0 and 2 * g + qc:
                            pe.wait_ge(acc_out, 2 * g + qc)
                        for h in range(HG):
                            last = nc.tensor.matmul(ps[h * QUAD:(h + 1) * QUAD, 4, j:], values[:, g % 2, kt, h, :],
                                                    prob[:, i % 2, h, j:], start=kt == 0, stop=kt == 4 * qc + 3)
                        last.then_inc(weighed, 1)

                    step = iter(range(GROUPS * len(PIECES)))
                    for g in range(GROUPS):
                        score(g, 0)
                        for i in range(NU):
                            between = UNIT_PIECES[i] // 3 if i + 1 < NU else 0
                            if i + 1 < NU:
                                score(g, i + 1, between)
                            weigh(g, i)
                            pieces(g, UNIT_PIECES[i] - 2 * between)
                            if i == ROWS_AFTER + 1:
                                maxima.pe_rows(pe, g)

                    pe.wait_ge(acc_out, 2 * GROUPS)
                    pe.wait_ge(raised, 2 * NU * GROUPS)
                    for half, g in finals:
                        last = nc.tensor.matmul(ps[g * QUAD:(g + 1) * QUAD, 0, :], k["pick_total"][:, half, :],
                                                summed[:, half, g, :], start=half == 0, stop=half == 1)
                    last.then_inc(totals, 1)
                    pe.wait_ge(inverted, 1)

                    def mix(u):
                        half, g = finals[u]
                        pe.wait_ge(even, u + 1)
                        nc.tensor.matmul(ps[:, (1, 4)[half], :], proj[:, g, :], evened[:, u % 2, :],
                                         start=g == 0, stop=g == GROUPS - 1).then_inc(projected, 1)

                    for u in range(len(finals)):
                        if u >= 2:
                            pe.wait_ge(even, u - 1)
                        nc.tensor.matmul(ps[:, 2 + u % 2, :], k["spread_total"][:, u, :], inverse_parts[:, :],
                                         start=True, stop=True).then_inc(spread, 1)
                        if u:
                            mix(u - 1)
                    mix(len(finals) - 1)

                @block.scalar
                def _(act):
                    for u in range(GROUPS * NU):
                        qc, kt, j = UNITS[u % NU]
                        for pair in range(2):
                            act.wait_ge(scored, 2 * u + pair + 1)
                            if u >= 2:
                                act.wait_ge(weighed, u - 1)
                            nc.scalar.activation(prob[:, u % 2, 2 * pair:2 * pair + 2, j:],
                                                 ps[:, 2 * pair:2 * pair + 2, j:], ACT.Exp, scale=scale).then_inc(raised, 1)

                @block.vector
                def _(dve):
                    step = iter(range(GROUPS * len(PIECES)))
                    for g in range(GROUPS):
                        for i in range(NU):
                            for _ in range(UNIT_PIECES[i]):
                                n = next(step)
                                maxima.dve_piece(dve, n, (n + AHEAD) % len(PIECES))
                            if i == ROWS_AFTER:
                                maxima.dve_rows(dve, g, g * len(PIECES) + LEFT)
                            if i in (3, NU - 1):
                                half = int(i > 3)
                                dve.wait_ge(weighed, g * NU + (4, NU)[half])
                                nc.vector.tensor_copy(summed[:, half, g, :], ps[:, 4, :]).then_inc(acc_out, 1)
                    dve.wait_ge(maxima.used, GROUPS * len(PIECES))
                    dve.wait_ge(totals, 1)
                    cut = Chain(dve, parted)
                    cut(nc.vector.reciprocal(inverse[:, :], ps[:, 0, :]))
                    in_parts(nc, k, cut, inverse[:, :], inverse_parts[:, :]).then_inc(inverted, 1)
                    dve.wait_ge(acc_out, 2 * GROUPS)
                    for u, (half, g) in enumerate(finals):
                        dve.wait_ge(spread, u + 1)
                        if u >= 2:
                            dve.wait_ge(projected, u - 1)
                        nc.vector.tensor_tensor(evened[:, u % 2, :], summed[:, half, g, :], ps[:, 2 + u % 2, :],
                                                ALU.mult).then_inc(even, 1)
                    for half in range(2):
                        at = bass.ds(b * L + half * CH, CH)
                        dve.wait_ge(projected, GROUPS * (half + 1))
                        if residual is not None:
                            nc.vector.tensor_tensor(out[:, at], ps[:, (1, 4)[half], :], residual[:, at],
                                                    ALU.add).then_inc(done, 1)
                        else:
                            nc.vector.tensor_copy(out[:, at], ps[:, (1, 4)[half], :]).then_inc(done, 1)
                    dve.wait_ge(done, 2)


def route(nc, ps, router, h, mask):
    with Stage(nc, "route") as st:
        logits, best, taken = st.sb("logits", [P, NT, E]), st.sb("best", [P, NT]), st.sb("taken", [P, NT])
        scored, chain = st.sem("scored"), st.sem("chain")
        with nc.Block() as block:

            @block.tensor
            def _(pe):
                for t in range(NT):
                    last = nc.tensor.matmul(ps[:, 0, t * E:(t + 1) * E], h[:, t * P:(t + 1) * P], router[:, :],
                                            start=True, stop=True)
                last.then_inc(scored, 1)

            @block.vector
            def _(dve):
                link = Chain(dve, chain)
                dve.wait_ge(scored, 1)
                link(nc.vector.tensor_copy(logits[:, :, :], ps[:, 0, 0:NT * E].rearrange("p (t e) -> p t e", e=E)))
                link(nc.vector.reduce_max(best[:, :], logits[:, :, :], AX_X))
                link(nc.vector.tensor_tensor(logits[:, :, :], logits[:, :, :],
                                             best[:, :].unsqueeze(2).to_broadcast([P, NT, E]), ALU.is_equal))
                link(nc.vector.tensor_copy(mask[:, :, 0], logits[:, :, 0]))
                link(nc.vector.tensor_copy(taken[:, :], logits[:, :, 0]))
                for e in range(1, E):
                    link(nc.vector.tensor_tensor(mask[:, :, e], logits[:, :, e], taken[:, :], ALU.is_gt))
                    link(nc.vector.tensor_tensor(taken[:, :], taken[:, :], logits[:, :, e], ALU.max))


def experts(nc, ps, k, wv, wp, h, mask, xa, s, x):
    FCH = DFF // P
    units = [(e, f) for e in range(E) for f in range(FCH)]
    with nc.Fori(0, NCH) as c, Stage(nc, "moe") as st:
        own = st.sb("own", [P, E, CH])
        gate = st.sb("gate", [P, 2, CH])
        act_v = st.sb("gated", [P, 2, CH])
        total = st.sb("total", [P, CH])
        spread, masked, gates, vals = (st.sem(n) for n in ("spread", "masked", "gates", "vals"))
        silus, gated, summed, chain, silu2 = (st.sem(n) for n in ("silus", "gated", "summed", "chain", "silu2"))
        with nc.Block() as block:

            @block.tensor
            def _(pe):
                for e in range(E):
                    if e >= 2:
                        pe.wait_ge(masked, e - 1)
                    for t in range(4):
                        col = mask[:, bass.ds(c * 4 + t, 1), e]
                        last = nc.tensor.matmul(ps[:, 6 + e % 2, t * P:(t + 1) * P], col.to_broadcast([P, P]),
                                                k["ident_b"][:, :], start=True, stop=True)
                    last.then_inc(spread, 1)

                def down(u):
                    e, f = units[u]
                    pe.wait_ge(gated, u + 1)
                    nc.tensor.matmul(ps[:, 4, :], wp[:, e, f, :], act_v[:, u % 2, :], start=u == 0,
                                     stop=u == len(units) - 1).then_inc(summed, 1)

                for u, (e, f) in enumerate(units):
                    pe.wait_ge(masked, e + 1)
                    if u >= 2:
                        pe.wait_ge(gated, u - 1)
                    nc.tensor.matmul(ps[:, u % 2, :], wv[:, e, f * P:(f + 1) * P], own[:, e, :],
                                     start=True, stop=True).then_inc(gates, 1)
                    nc.tensor.matmul(ps[:, 2 + u % 2, :], wv[:, e, DFF + f * P:DFF + (f + 1) * P], own[:, e, :],
                                     start=True, stop=True).then_inc(vals, 1)
                    if u:
                        down(u - 1)
                down(len(units) - 1)

            @block.scalar
            def _(act):
                for u in range(len(units)):
                    act.wait_ge(gates, u + 1)
                    if u >= 2:
                        act.wait_ge(gated, u - 1)
                    nc.scalar.activation(gate[:, u % 2, :], ps[:, u % 2, :], ACT.Silu).then_inc(silus, 1)
                act.wait_ge(chain, 1)
                nc.scalar.activation(total[:, :], total[:, :], ACT.Silu).then_inc(silu2, 1)

            @block.vector
            def _(dve):
                for e in range(E):
                    dve.wait_ge(spread, e + 1)
                    nc.vector.tensor_tensor(own[:, e, :], h[:, bass.ds(c * CH, CH)], ps[:, 6 + e % 2, :],
                                            ALU.mult).then_inc(masked, 1)
                for u in range(len(units)):
                    dve.wait_ge(silus, u + 1)
                    dve.wait_ge(vals, u + 1)
                    if u >= 2:
                        dve.wait_ge(summed, u - 1)
                    nc.vector.tensor_tensor(act_v[:, u % 2, :], gate[:, u % 2, :], ps[:, 2 + u % 2, :],
                                            ALU.mult).then_inc(gated, 1)
                at = bass.ds(c * CH, CH)
                dve.wait_ge(summed, len(units))
                nc.vector.tensor_tensor(total[:, :], xa[:, at], ps[:, 4, :], ALU.add).then_inc(chain, 1)
                dve.wait_ge(silu2, 1)
                nc.vector.tensor_tensor(total[:, :], total[:, :], s[:, at], ALU.mult).then_inc(chain, 1)
                dve.wait_ge(chain, 2)
                nc.vector.tensor_tensor(x[:, at], x[:, at], total[:, :], ALU.add).then_inc(chain, 1)
                dve.wait_ge(chain, 3)

NCHUNKS = len(DCH)
HALF = NT // 2
MAX_BANKS = ((7, 4), (7, 4), (2, 3), (2, 3))
NORM_BANKS = (4, 7)
BEFORE = ("v0", "v1", "s0", "s1", "v2", "v3", "s2", "s3", "v4", "m0", "m1", "v5", "v6", "m2", "m3", "v7")
DURING = {0: "s4", 1: "s5", 2: "s6", 3: "s7", 5: "m4", 6: "m5", 7: "m6", 8: "m7", 11: "r1"}
SCALAR_BEFORE = ("v0", "v1", "v2", "l0", "l1", "v3", "v4", "l2", "l3", "v5", "v6", "v7")
SCALAR_DURING = {1: ("l4",), 2: ("l5", "l6"), 3: ("l7",)}
VECTOR_BEFORE = ("i6", "n0", "n1", "j0", "j1", "j2", "n2", "n3", "m0", "m1", "j3", "j4", "m2", "m3", "r0", "j5", "j6")
VECTOR_DURING = {0: (("n4", "n5", "n6", "n7"), ("m4", "m5"), ()), 1: ((), ("m6", "m7"), ("r1",))}


def shift_tokens(nc, name, x, out, also=None):
    with Stage(nc, name) as st:
        copied, loaded = st.sem("copied"), st.sem("loaded")
        half = C // 2
        xv = x[:, :].rearrange("p (b t) -> p b t", b=B)
        ov = out[:, :].rearrange("p (b t) -> p b t", b=B)
        with nc.Block() as block:

            @block.scalar
            def _(act):
                nc.scalar.activation(out[0:half, :], x[0:half, :], ACT.Copy).then_inc(copied, 1)
                act.wait_ge(copied, 1)

            @block.vector
            def _(dve):
                nc.vector.tensor_copy(ov[half:, :, 1:], xv[half:, :, :L - 1]).then_inc(loaded, 1)
                nc.vector.memset(ov[half:, :, 0:1], 0.0).then_inc(loaded, 1)
                dve.wait_ge(loaded, 2)


def load_layer(nc, layer, pairs, tables, scales):
    with Stage(nc, "layer") as st:
        loaded, scaled = st.sem("loaded"), st.sem("scaled")
        with nc.Block() as block:

            @block.sync
            def _(sp):
                for dst, src in pairs:
                    sp.dma_start(dst, src[bass.ds(layer, 1)].squeeze(0)).then_inc(loaded, 16)
                for dst, src in tables:
                    sp.dma_start(dst[:, :], src).then_inc(loaded, 16)
                sp.wait_ge(loaded, 16 * (len(pairs) + len(tables)))

            @block.vector
            def _(dve):
                dve.wait_ge(loaded, 16 * (len(pairs) + len(tables)))
                for n, (dst, _) in enumerate(tables):
                    nc.vector.tensor_scalar(dst[:, :], dst[:, :], scales[:, n:n + 1], None, ALU.mult).then_inc(scaled, 1)
                dve.wait_ge(scaled, len(tables))


def local_pairs(nc, name, ps, k, weights, w_dram, first, count, xs, tables, buf, cur):
    NQ = 2 * NCH
    TWOS = NT // 2
    qk, low, values = buf["qk"], buf["low"], buf["values"]
    square, part, sine = buf["square"], buf["part"], buf["sine"]
    prob, inverse, head_out = buf["prob"], buf["inverse"], buf["head_out"]
    norm, norm_parts, top, neg_parts = buf["norm"], buf["norm_parts"], buf["top"], buf["neg_parts"]
    with Stage(nc, name) as st:
        S = lambda *names: [st.sem(n) for n in names]
        cleared, zeroed, fetched, projected, squared, bank_used, sined, added = S(
            "cleared", "zeroed", "fetched", "projected", "squared", "bank_used", "sined", "added")
        norms, rooted, parted, inverted, spread, normed, lowered = S(
            "norms", "rooted", "parted", "inverted", "spread", "normed", "lowered")
        v_projected, v_out, max_scored, max_used, neg, rows, rows_out = S(
            "v_projected", "v_out", "max_scored", "max_used", "neg", "rows", "rows_out")
        scored, raised, weighed, recip, evened, mixed, done = S(
            "scored", "raised", "weighed", "recip", "evened", "mixed", "done")
        head = lambda h: slice(h * DH, (h + 1) * DH)
        last_of = lambda t: t % TILES == TILES - 1
        span = lambda t: P if last_of(t) else SPAN
        with nc.Block() as block:

            @block.sync
            def _(sp):
                for v in range(count):
                    if v:
                        sp.wait_ge(mixed, v * NCH)
                    sp.dma_start(weights[(v + 1) % 2][:, :, :],
                                 w_dram[bass.ds(first + v + 1, 1)].squeeze(0)).then_inc(fetched, 16)
                sp.wait_ge(fetched, 16 * count)

            @block.tensor
            def _(pe):
                def project(v, i):
                    c, n = divmod(i, 2)
                    if i >= 2:
                        pe.wait_ge(squared, v * NQ + i - 1)
                        pe.wait_ge(bank_used, v * NQ + i - 1)
                    for s in range(2):
                        last = nc.tensor.matmul(ps[:, 2 * n + s, :], weights[v % 2][:, 2 * n + s, :], xs[:, chunk(c)],
                                                start=True, stop=True)
                    last.then_inc(projected, 1)

                def norm(v, i):
                    pe.wait_ge(squared, v * NQ + i + 1)
                    q = i % 4 * QUAD
                    nc.tensor.matmul(ps[q:q + QUAD, NORM_BANKS[i // 8], :], k["norm_row"][:, i // 4 % 2, :],
                                     square[:, i % 2, :], start=i // 4 % 2 == 0, stop=i // 4 % 2 == 1).then_inc(norms, 1)

                def project_values(v, c):
                    if c >= 2:
                        pe.wait_ge(v_out, v * NCH + c - 1)
                    for t in range(4):
                        a = c * CH + t * P
                        last = nc.tensor.matmul(ps[:, 5 + c % 2, t * P:(t + 1) * P], xs[:, a:a + P],
                                                weights[v % 2][:, 4, :], start=True, stop=True)
                    last.then_inc(v_projected, 1)

                def spread_norms(v, pair):
                    pe.wait_ge(inverted, 2 * v + pair // 4 + 1)
                    for i in (2 * pair, 2 * pair + 1):
                        if i < 4:
                            pe.wait_ge(bank_used, (v + 1) * NQ)
                        elif i < 8:
                            pe.wait_ge(normed, v * NQ + i - 3)
                        else:
                            pe.wait_ge(normed, v * NQ + i - 1)
                        bank = i if i < 4 else i - 4 if i < 8 else 2 + i % 2
                        nc.tensor.matmul(ps[:, bank, :], k["norm_spread"][:, i % 8, :], norm_parts[:, i // 8, :],
                                         start=True, stop=True).then_inc(spread, 1)

                def maxima(v, n):
                    g, h = divmod(n, 2)
                    if h == 0:
                        if g == 0:
                            pe.wait_ge(rooted, 4 * v + 3)
                        elif g == 2:
                            pe.wait_ge(normed, (v + 1) * NQ)
                        pe.wait_ge(lowered, v * NQ + 4 * (g + 1))
                    if g % 2 == 1:
                        pe.wait_ge(max_used, 2 * (v * B + g - 1) + h + 1)
                    bank = MAX_BANKS[g][h]
                    nc.tensor.matmul(ps[:, bank, :], k["ident_b"][:, :], k["band_q"][:, :], start=True, stop=True)
                    for j in range(TILES):
                        for win in range(4):
                            at = g * L + j * P + win * WIN
                            back = 0 if j == 0 and win == 0 else WIN
                            last = nc.tensor.matmul(
                                ps[win * WIN:(win + 1) * WIN, bank, j * 2 * WIN + WIN - back:(j + 1) * 2 * WIN],
                                low[head(h), 0, at:at + WIN], low[head(h), 1, at - back:at + WIN],
                                start=False, stop=True, skip_group_check=True)
                    last.then_inc(max_scored, 1)

                def turn(v, half):
                    pe.wait_ge(neg, 8 * v + 4 * (half + 1))
                    pe.wait_ge(cleared, 3)
                    nc.tensor.matmul(ps[0:2 * NT, 2, 0:P], neg_parts[:, half, 0:2 * NT], k["ident_b"][:, :],
                                     start=True, stop=True)
                    nc.tensor.matmul(ps[0:2 * NT, 2, P:SPAN], neg_parts[:, half, 1:2 * NT + 1], k["ident_b"][:, 0:WIN],
                                     start=True, stop=True).then_inc(rows, 1)

                def score(v, two):
                    if two > 0:
                        pe.wait_ge(raised, v * TWOS + two)
                    for h in range(2):
                        out = ps[:, h, 0:2 * SEEN].rearrange("p (j n) -> p j n", j=2)
                        nc.tensor.matmul(out, k["ident_b"][:, :], k["band_k"][:, :].unsqueeze(1).to_broadcast([P, 2, SEEN]),
                                         start=True, stop=True)
                        for j in range(2):
                            t = 2 * two + j
                            for at in (0, DH):
                                n = min(SEEN, span(t) - at)
                                nc.tensor.matmul(out[at:at + DH, j, 0:n], qk[head(h), 1, t * P + at:t * P + at + DH],
                                                 qk[head(h), 0, t * P + at:t * P + at + n], start=False, stop=True,
                                                 skip_group_check=True)
                        if two > 0:
                            subtract(v, two, h)

                def subtract(v, two, h):
                    half = 2 * two // HALF
                    if two * 2 % HALF == 0 and h == 0:
                        pe.wait_ge(rows_out, 2 * v + half + 1)
                    out = ps[:, h, 0:2 * SEEN].rearrange("p (j n) -> p j n", j=2)
                    for j in range(2):
                        u = h * HALF + (2 * two + j) % HALF
                        for at in (0, DH):
                            n = min(SEEN, span(2 * two + j) - at)
                            last = nc.tensor.matmul(out[at:at + DH, j, 0:n], k["unit_row"][:, u:u + 1].to_broadcast([P, DH]),
                                                    buf["rows"][:, half, at:at + n], start=False, stop=True,
                                                    skip_group_check=True)
                    if h == 1:
                        last.then_inc(scored, 1)

                def weigh(v, t):
                    c, j = divmod(t, 4)
                    pe.wait_ge(raised, v * TWOS + t // 2 + 1)
                    if j == 0 and c >= 2:
                        pe.wait_ge(done, v * NCH + c - 1)
                    pieces = [(c, j * P, 0, min(span(t), CH - j * P))]
                    if pieces[0][3] < span(t):
                        pieces.append((c + 1, 0, P, span(t) - P))
                    for cc, to, frm, n in pieces:
                        if cc > c >= 1:
                            pe.wait_ge(done, v * NCH + c)
                        opens = to == 0 and (j == 0 and c % 2 == 0 or cc > c)
                        for what, bank in ((None, 4), ("ones", 6)):
                            for h in range(2):
                                left = values[:, t, head(h)] if what is None else k["ones"][:, :]
                                last = nc.tensor.matmul(ps[head(h), bank + cc % 2, to:to + n], left,
                                                        prob[:, t // 2 % 2, h, t % 2, frm:frm + n], start=opens,
                                                        stop=True, skip_group_check=True)
                    last.then_inc(weighed, 1)

                def mix(v, c):
                    pe.wait_ge(evened, v * NCH + c + 1)
                    nc.tensor.matmul(ps[:, 6 + c % 2, :], weights[v % 2][:, 5, :], head_out[:, c % 2, :], start=True,
                                     stop=True).then_inc(mixed, 1)

                for v in range(count):
                    if v:
                        pe.wait_ge(fetched, 16 * v)
                        pe.wait_ge(raised, v * TWOS)
                    for i in range(NQ):
                        project(v, i)
                        if i == 1 and v:
                            mix(v - 1, NCH - 1)
                            pe.wait_ge(done, v * NCH)
                        if i:
                            norm(v, i - 1)
                    norm(v, NQ - 1)
                    steps = {"v": project_values, "s": spread_norms, "m": maxima, "r": turn}
                    for step in BEFORE:
                        steps[step[0]](v, int(step[1]))
                    pe.wait_ge(normed, v * NQ + NQ // 2)
                    score(v, 0)
                    turn(v, 0)
                    for h in range(2):
                        subtract(v, 0, h)
                    for t in range(NT):
                        if t == 0:
                            pe.wait_ge(v_out, (v + 1) * NCH)
                            pe.wait_ge(max_used, 2 * (v * B + 2))
                        if t % 2 == 0 and t + 2 < NT:
                            score(v, t // 2 + 1)
                        weigh(v, t)
                        if t >= 4 and t % 4 == 2:
                            mix(v, t // 4 - 1)
                        if t in DURING:
                            steps[DURING[t][0]](v, int(DURING[t][1]))
                mix(count - 1, NCH - 1)

            @block.scalar
            def _(act):
                def lower(v, pair):
                    for i in (2 * pair, 2 * pair + 1):
                        c, n = divmod(i, 2)
                        act.wait_ge(normed, v * NQ + i + 1)
                        nc.scalar.activation(low[:, n, chunk(c)], qk[:, n, chunk(c)], ACT.Copy).then_inc(lowered, 1)

                for v in range(count):
                    for i in range(NQ):
                        act.wait_ge(projected, v * NQ + i + 1)
                        if v * NQ + i >= 2:
                            act.wait_ge(norms, v * NQ + i - 1)
                        nc.scalar.activation(square[:, i % 2, :], ps[:, i % 2 * 2, :], ACT.Square).then_inc(squared, 1)
                        if i in (NQ // 2, NQ - 1):
                            half = i // (NQ - 1)
                            act.wait_ge(norms, v * NQ + (half + 1) * NQ // 2)
                            if v or half:
                                act.wait_ge(inverted, 2 * v + half)
                            nc.scalar.activation(norm[:, :], ps[:, NORM_BANKS[half], :], ACT.Sqrt).then_inc(rooted, 1)
                    for step in SCALAR_BEFORE:
                        if step[0] == "v":
                            c = int(step[1])
                            act.wait_ge(v_projected, v * NCH + c + 1)
                            nc.scalar.activation(values[:, 4 * c:4 * c + 4, :],
                                                 ps[:, 5 + c % 2, :].rearrange("p (t n) -> p t n", n=P),
                                                 ACT.Copy).then_inc(v_out, 1)
                        else:
                            lower(v, int(step[1]))
                    for two in range(TWOS):
                        act.wait_ge(scored, v * TWOS + two + 1)
                        if two >= 2:
                            act.wait_ge(weighed, v * NT + 2 * (two - 1))
                        s = ps[:, 0:2, 0:2 * SEEN].rearrange("p h (j n) -> p h j n", j=2)
                        if v == 0 and two == 0:
                            act.wait_ge(zeroed, 1)
                        for at, js in [(0, (0, 2)), (DH, (0, 2))] if not last_of(2 * two + 1) else \
                                [(0, (0, 2)), (DH, (0, 1)), (DH, (1, 2))]:
                            n = min(SEEN, span(2 * two + js[1] - 1) - at)
                            last = nc.scalar.activation(prob[at:at + DH, two % 2, :, js[0]:js[1], at:at + n],
                                                        s[at:at + DH, :, js[0]:js[1], 0:n], ACT.Exp, scale=QK_SCALE)
                        last.then_inc(raised, 1)
                        for step in SCALAR_DURING.get(two, ()):
                            lower(v, int(step[1]))

            @block.gpsimd
            def _(pool):
                nc.gpsimd.memset(prob[:, :, :, :, :], 0.0).then_inc(zeroed, 1)
                pool.wait_ge(zeroed, 1)
                for i in range(count * NQ):
                    c, n = divmod(i % NQ, 2)
                    pool.wait_ge(sined, i + 1)
                    pool.wait_ge(bank_used, i + 1)
                    if i:
                        pool.wait_ge(added, i)
                    nc.gpsimd.tensor_tensor(qk[:, n, chunk(c)], part[:, i % 2, :], sine[:, i % 2, :],
                                            ALU.add).then_inc(added, 1)

            @block.vector
            def _(dve):
                cut, link = Chain(dve, parted), Chain(dve, neg)
                nc.vector.memset(buf["rows"][2 * NT:, :, :], 0.0).then_inc(cleared, 1)
                for half in range(2):
                    nc.vector.memset(neg_parts[:, half, 2 * NT:], 0.0).then_inc(cleared, 1)

                def maxima(v, n):
                    g, h = divmod(n, 2)
                    at = (g % 2) * TILES
                    dve.wait_ge(max_scored, 2 * v * B + n + 1)
                    nc.vector.reduce_max(top[:, g // 2, h * HALF + at:h * HALF + at + TILES],
                                         ps[:, MAX_BANKS[g][h], :].rearrange("p (u n) -> p u n", n=2 * WIN),
                                         AX_X).then_inc(max_used, 1)

                def turn(v, half):
                    dve.wait_ge(max_used, 2 * v * B + B * (half + 1))
                    t, turned = top[:, half, :], buf["rows"][0:2 * NT, half, :]
                    parts = neg_parts[:, half, 0:2 * NT].rearrange("p (s u) -> p s u", s=2)
                    link(nc.vector.tensor_scalar(t, t, -1.0, None, ALU.mult))
                    link(nc.vector.tensor_copy(parts[:, 0, :], t))
                    link(nc.vector.tensor_tensor(t, t, parts[:, 0, :], ALU.subtract))
                    link(nc.vector.tensor_copy(parts[:, 1, :], t))
                    dve.wait_ge(rows, 2 * v + half + 1)
                    nc.vector.tensor_copy(turned, ps[0:2 * NT, 2, 0:SPAN]).then_inc(rows_out, 1)

                def invert(v, half, piece):
                    parts, columns = norm_parts[:, half, :], slice((piece - 1) * P, piece * P)
                    if piece == 0:
                        dve.wait_ge(rooted, 4 * v + 2 * half + 1)
                        nc.vector.tensor_scalar(norm[:, :], norm[:, :], 1e-12, None, ALU.max).then_inc(rooted, 1)
                        dve.wait_ge(rooted, 4 * v + 2 * half + 2)
                    elif piece < 5:
                        cut(nc.vector.reciprocal(norm[:, columns], norm[:, columns]))
                    elif piece == 5:
                        cut(nc.vector.tensor_copy(parts, norm[:, :]))
                        cut(nc.vector.scalar_tensor_tensor(out=norm[:, :], in0=parts, scalar=k["minus_first"][:, 0:1],
                                                           in1=norm[:, :], op0=ALU.mult, op1=ALU.add))
                    else:
                        cut(nc.vector.tensor_copy(parts, norm[:, :]))
                        nc.vector.scalar_tensor_tensor(out=parts, in0=parts, scalar=k["minus_second"][:, 0:1],
                                                       in1=norm[:, :], op0=ALU.mult, op1=ALU.add).then_inc(inverted, 1)

                def normalise(v, pair):
                    for i in (2 * pair, 2 * pair + 1):
                        c, n = divmod(i, 2)
                        bank = i if i < 4 else i - 4 if i < 8 else 2 + i % 2
                        if i == 0:
                            dve.wait_ge(added, (v + 1) * NQ)
                        dve.wait_ge(spread, v * NQ + i + 1)
                        nc.vector.tensor_tensor(qk[:, n, chunk(c)], qk[:, n, chunk(c)], ps[:, bank, :],
                                                ALU.mult).then_inc(normed, 1)

                def do(v, step):
                    what, n = step[0], int(step[1])
                    if what in "ij":
                        invert(v, "ij".index(what), n)
                    else:
                        {"n": normalise, "m": maxima, "r": turn}[what](v, n)

                for v in range(count):
                    for i in range(v * NQ, (v + 1) * NQ):
                        if i % NQ >= 10:
                            invert(v, 0, i % NQ - 10)
                        c, n = divmod(i % NQ, 2)
                        at = slice(c % 2 * CH, (c % 2 + 1) * CH)
                        dve.wait_ge(projected, i + 1)
                        if i >= 2:
                            dve.wait_ge(added, i - 1)
                        nc.vector.tensor_tensor(sine[:, i % 2, :], ps[:, 2 * n + 1, :], tables[2 * n + 1][:, at],
                                                ALU.mult).then_inc(sined, 1)
                        dve.wait_ge(squared, i + 1)
                        nc.vector.tensor_tensor(part[:, i % 2, :], ps[:, 2 * n, :], tables[2 * n][:, at],
                                                ALU.mult).then_inc(bank_used, 1)
                    for step in VECTOR_BEFORE:
                        do(v, step)
                    for c in range(NCH):
                        extra = VECTOR_DURING.get(c, ((), (), ()))
                        for step in extra[0]:
                            do(v, step)
                        dve.wait_ge(weighed, v * NT + 4 * c + 4)
                        if v * NCH + c:
                            dve.wait_ge(evened, v * NCH + c)
                        nc.vector.reciprocal(inverse[:, :], ps[:, 6 + c % 2, :]).then_inc(recip, 1)
                        dve.wait_ge(recip, v * NCH + c + 1)
                        nc.vector.tensor_tensor(head_out[:, c % 2, :], ps[:, 4 + c % 2, :], inverse[:, :],
                                                ALU.mult).then_inc(evened, 1)
                        for step in extra[1]:
                            do(v, step)
                        dve.wait_ge(mixed, v * NCH + c + 1)
                        nc.vector.tensor_tensor(cur[:, chunk(c)], cur[:, chunk(c)], ps[:, 6 + c % 2, :],
                                                ALU.add).then_inc(done, 1)
                        for step in extra[2]:
                            do(v, step)
                dve.wait_ge(done, count * NCH)


def gated_network(nc, ps, xn, w1, w2, b1, b2, cur):
    units = [(c, f) for c in range(NCH) for f in range(NCHUNKS)]
    with Stage(nc, "gn") as st:
        gate, product = st.sb("gate", [P, 2, CH]), st.sb("product", [P, 2, CH])
        lefts, gates, gelus, gated, summed, done = (st.sem(n) for n in ("lefts", "gates", "gelus", "gated", "summed", "done"))
        def finish(dve, c):
            dve.wait_ge(summed, NCHUNKS * (c + 1))
            nc.vector.scalar_tensor_tensor(out=cur[:, chunk(c)], in0=ps[:, 4 + c % 2, :], scalar=b2,
                                           in1=cur[:, chunk(c)], op0=ALU.add, op1=ALU.add).then_inc(done, 1)

        with nc.Block() as block:

            @block.tensor
            def _(pe):
                def down(u):
                    c, f = units[u]
                    m = DCH[f][1]
                    pe.wait_ge(gated, u + 1)
                    if f == 0 and c >= 2:
                        pe.wait_ge(done, c - 1)
                    nc.tensor.matmul(ps[:, 4 + c % 2, :], w2[0:m, f, :], product[0:m, u % 2, :], start=f == 0,
                                     stop=f == NCHUNKS - 1).then_inc(summed, 1)

                for u, (c, f) in enumerate(units):
                    o, m = DCH[f]
                    if u >= 2:
                        pe.wait_ge(gated, u - 1)
                    nc.tensor.matmul(ps[0:m, u % 2, :], w1[:, DI + o:DI + o + m], xn[:, chunk(c)],
                                     start=True, stop=True).then_inc(gates, 1)
                    nc.tensor.matmul(ps[0:m, 2 + u % 2, :], w1[:, o:o + m], xn[:, chunk(c)],
                                     start=True, stop=True).then_inc(lefts, 1)
                    if u:
                        down(u - 1)
                down(len(units) - 1)

            @block.scalar
            def _(act):
                for u, (c, f) in enumerate(units):
                    m = DCH[f][1]
                    act.wait_ge(gates, u + 1)
                    if u >= 2:
                        act.wait_ge(gated, u - 1)
                    nc.scalar.activation(gate[0:m, u % 2, :], ps[0:m, u % 2, :], ACT.Gelu,
                                         bias=b1[0:m, NCHUNKS + f:NCHUNKS + f + 1]).then_inc(gelus, 1)

            @block.vector
            def _(dve):
                for u, (c, f) in enumerate(units):
                    m = DCH[f][1]
                    dve.wait_ge(gelus, u + 1)
                    dve.wait_ge(lefts, u + 1)
                    if u >= 2:
                        dve.wait_ge(summed, u - 1)
                    nc.vector.scalar_tensor_tensor(out=product[0:m, u % 2, :], in0=ps[0:m, 2 + u % 2, :],
                                                   scalar=b1[0:m, f:f + 1], in1=gate[0:m, u % 2, :],
                                                   op0=ALU.add, op1=ALU.mult).then_inc(gated, 1)
                    if f == 1 and c:
                        finish(dve, c - 1)
                finish(dve, NCH - 1)
                dve.wait_ge(done, NCH)


IN_STAGE = 4


def gate_and_store(nc, ps, x, s, g, out):
    with Stage(nc, "end") as st:
        silus, products, sums, stored = (st.sem(n) for n in ("silus", "products", "sums", "stored"))
        with nc.Block() as block:

            @block.scalar
            def _(act):
                for c in range(NCH):
                    nc.scalar.activation(g[:, chunk(c)], g[:, chunk(c)], ACT.Silu).then_inc(silus, 1)

            @block.vector
            def _(dve):
                for c in range(NCH):
                    dve.wait_ge(silus, c + 1)
                    nc.vector.tensor_tensor(s[:, chunk(c)], s[:, chunk(c)], g[:, chunk(c)], ALU.mult).then_inc(products, 1)
                    dve.wait_ge(products, c + 1)
                    nc.vector.tensor_tensor(x[:, chunk(c)], x[:, chunk(c)], s[:, chunk(c)], ALU.add).then_inc(sums, 1)

            @block.sync
            def _(sp):
                for c in range(NCH):
                    sp.wait_ge(sums, c + 1)
                    sp.dma_start(out[:, chunk(c)], x[:, chunk(c)]).then_inc(stored, 16)
                sp.wait_ge(stored, 16 * NCH)


def build_program(nc, a, out):
    with ExitStack() as whole:
        def buffers(ctx, names):
            return {n: ctx.enter_context(nc.sbuf_tensor("sb_" + n, list(a[n].shape), a[n].dtype)) for n in names}

        def loads(tensors):
            return [(t[:], a[n]) for n, t in tensors.items()]

        ps = whole.enter_context(nc.psum_tensor("ps", [P, 8, CH], F32))
        k = buffers(whole, CONSTANTS)
        x, s, cur = (whole.enter_context(nc.sbuf_tensor(n, [P, T], F32)) for n in ("x", "s", "cur"))
        q_parts, k_parts = (nc.dram_tensor(n, [3, C, T + L], BF16).ap() for n in ("q_parts", "k_parts"))

        with ExitStack() as ctx:
            w = buffers(ctx, [n for n in a if n.startswith("ta_") and n != "ta_bv"])
            w["ta_bv"] = ctx.enter_context(nc.sbuf_tensor("sb_ta_bv", [P, P], F32))
            load_constants(nc, loads(k) + [(x[:, :], a["x"])] +
                           [(t[:], a[n].to_broadcast([P, P]) if n == "ta_bv" else a[n]) for n, t in w.items()])
            layernorm(nc, "ln0", ps, k, x, cur)
            tile_attention(nc, ps, k, w, cur, s)

        with ExitStack() as ctx:
            vtok = ctx.enter_context(nc.sbuf_tensor("vtok0", [P, NT, P], F32))
            w = buffers(ctx, ["cq", "ck", "cv", "cqs", "cks", "cproj", "taps", "ln1"])
            with ExitStack() as inner:
                h, mixed = (inner.enter_context(nc.sbuf_tensor(n, [P, T], F32)) for n in ("h0", "h_mixed"))
                tables = buffers(inner, ["cos", "sin"])
                load_constants(nc, loads(w) + loads(tables))
                layernorm(nc, "ln1", ps, k, cur, h, w["ln1"][:, 0:1], w["ln1"][:, 1:2])
                causal_convolution(nc, w["taps"], h, mixed)
                causal_inputs(nc, "ci0", ps, mixed, dict(q=w["cq"], k=w["ck"], v=w["cv"], q_swapped=w["cqs"],
                                                         k_swapped=w["cks"]), tables, q_parts, k_parts, vtok)
            causal_attention(nc, "ca0", ps, k, q_parts, k_parts, vtok, w["cproj"], cur, cur)
        with ExitStack() as ctx:
            h = ctx.enter_context(nc.sbuf_tensor("h1", [P, T], F32))
            mask = ctx.enter_context(nc.sbuf_tensor("mask", [P, NT, E], BF16))
            w = buffers(ctx, ["wv", "wp", "router", "ln2"])
            load_constants(nc, loads(w))
            layernorm(nc, "ln2", ps, k, cur, h, w["ln2"][:, 0:1], w["ln2"][:, 1:2])
            route(nc, ps, w["router"], h, mask)
            experts(nc, ps, k, w["wv"], w["wp"], h, mask, cur, s, x)

        with ExitStack() as ctx:
            vtok = ctx.enter_context(nc.sbuf_tensor("vtok1", [P, NT, P], F32))
            w = buffers(ctx, ["dq", "dk", "dv", "dproj"])
            load_constants(nc, loads(w))
            layernorm(nc, "ln3", ps, k, x, cur)
            causal_inputs(nc, "ci1", ps, cur, dict(q=w["dq"], k=w["dk"], v=w["dv"]), None, q_parts, k_parts, vtok)
            causal_attention(nc, "ca1", ps, k, q_parts, k_parts, vtok, w["dproj"], s, None)

        with ExitStack() as ctx:
            sb = lambda n, shape, dt=F32: ctx.enter_context(nc.sbuf_tensor(n, shape, dt))
            xs = sb("shifted", [P, T])
            tables = [sb(f"table{n}", [P, L]) for n in range(4)]
            pair_w = [sb(f"pair_w{n}", [P, 6, P]) for n in range(2)]
            scales, w1, w2 = sb("scales", [P, 4]), sb("w1", [P, 2 * DI]), sb("w2", [P, NCHUNKS, C])
            b1, small = sb("b1", [P, 2 * NCHUNKS]), sb("small", [P, 3])
            load_constants(nc, [(pair_w[0][:], a["pair_w"][0])])
            with nc.Fori(0, LAYERS) as layer:
                load_layer(nc, layer, [(scales[:], a["scales"]), (w1[:], a["w1"]), (w2[:], a["w2"]), (b1[:], a["b1"]),
                                       (small[:], a["small"])], [(t, a[f"table{n}"]) for n, t in enumerate(tables)],
                           scales)
                shift_tokens(nc, "shift1", cur, xs)
                with ExitStack() as inner:
                    new = lambda n, shape, dt=F32: inner.enter_context(nc.sbuf_tensor("pair_" + n, shape, dt))
                    buf = dict(qk=new("qk", [P, 2, T]), low=new("low", [P, 2, T], BF16), values=new("values", [P, NT, P]),
                               square=new("square", [P, 2, CH]), part=new("part", [P, 2, CH]), sine=new("sine", [P, 2, CH]),
                               prob=new("prob", [P, 2, 2, 2, SPAN]), inverse=new("inverse", [P, CH]),
                               head_out=new("head_out", [P, 2, CH]), norm=new("norm", [P, CH]), top=new("top", [P, 2, NT]),
                               neg_parts=new("neg_parts", [P, 2, 2 * NT + 1], BF16), rows=new("rows", [P, 2, SPAN], BF16),
                               norm_parts=new("norm_parts", [P, 2, CH], BF16))
                    with nc.Fori(0, PAIRS // IN_STAGE) as part:
                        local_pairs(nc, "pairs", ps, k, pair_w, a["pair_w"], layer * PAIRS + part * IN_STAGE, IN_STAGE,
                                    xs, tables, buf, cur)
                shift_tokens(nc, "shift2", cur, xs)
                with nc.sbuf_tensor("normed", [P, T], F32) as normed:
                    layernorm(nc, "ln4", ps, k, xs, normed, small[:, 0:1], small[:, 1:2])
                    gated_network(nc, ps, normed, w1, w2, b1, small[:, 2:3], cur)
        gate_and_store(nc, ps, x, s, cur, out)


CONSTANTS = ["ident", "ident_b", "mean", "mean_row", "pick_row", "after_q", "after_k", "pick_total", "spread_total",
             "norm_row", "norm_spread", "band_q", "band_k", "unit_row", "ones",
             "minus_first", "minus_second"]


def constants():
    f, bf = np.float32, mybir.dt.np(BF16)
    c = {"ident": np.eye(P, dtype=f), "ident_b": np.eye(P).astype(bf), "mean": np.full((P, P), 1.0 / C, f),
         "ones": np.ones((P, DH), f)}
    c["mean_row"], c["pick_row"] = np.zeros((P, 2, QUAD), f), np.zeros((P, NCH, P), f)
    for j in range(2):
        c["mean_row"][:, j, j] = 1.0 / C
    for i in range(NCH):
        c["pick_row"][i % 4 * QUAD + i // 4, i, :] = 1
    at = np.arange(P)
    c["after_q"] = np.where(at[None, :] > at[:, None], MASKED, 0).astype(bf)
    c["after_k"] = np.ascontiguousarray(c["after_q"].T)
    row = at % QUAD
    c["pick_total"], c["spread_total"] = np.zeros((P, 2, QUAD), f), np.zeros((P, 2 * GROUPS, P), bf)
    for half in range(2):
        for h in range(HG):
            holds = (row // HG % 2 == half) & (row % HG == h)
            c["pick_total"][h * QUAD + HD, half, holds[:QUAD]] = 1
            for g in range(GROUPS):
                rows = np.flatnonzero(holds & (at // QUAD == g) & (row < 24))
                c["spread_total"][rows[:, None], half * GROUPS + g, np.arange(h * QUAD, (h + 1) * QUAD)[None]] = 1
    c["norm_row"], c["norm_spread"] = np.zeros((P, 2, QUAD), f), np.zeros((P, NCH, P), bf)
    for h in range(2):
        for part in range(3):
            for j in range(2):
                c["norm_row"][h * DH:(h + 1) * DH, j, 8 * part + 2 * j + h] = 1
            for i in range(NCH):
                c["norm_spread"][i % 4 * QUAD + 8 * part + 2 * (i // 4) + h, i, h * DH:(h + 1) * DH] = 1
    part = at % QUAD // 8
    c["minus_first"], c["minus_second"] = -(part >= 1).astype(f)[:, None], -(part == 2).astype(f)[:, None]
    q, key = at % WIN, np.arange(2 * WIN) - WIN
    seen = (key[None, :] <= q[:, None]) & (key[None, :] >= q[:, None] - WIN)
    band = np.tile(np.where(seen, 0, MASKED)[:, None, :], (1, TILES, 1))
    band[:WIN, 0, :WIN] = MASKED
    c["band_q"] = band.reshape(P, TILES * 2 * WIN).astype(bf)
    ahead = np.arange(SEEN)[None, :] - at[:, None] % DH
    c["band_k"] = np.where((ahead >= 0) & (ahead <= WIN), 0, MASKED).astype(bf)
    c["unit_row"] = np.concatenate([np.eye(NT), np.eye(NT), np.zeros((P - 2 * NT, NT))]).astype(bf)
    inv = (1.0 / f(10000.0) ** (np.arange(0, HD, 2, dtype=f) / HD)).astype(f)
    angle = np.tile(np.arange(L, dtype=f)[None, :] * inv[:, None], (2, 1))
    sign = np.repeat(np.array([-1, 1], f), HD // 2)[:, None]
    c["cos"] = np.tile(np.cos(angle), (HEADS, 1)).astype(f)
    c["sin"] = np.tile(np.sin(angle) * sign, (HEADS, 1)).astype(f)
    half = np.arange(0, DH, 2, dtype=f)
    inv = (f(1.0) / f(10000.0) ** (half / f(DH))).astype(f)
    t = np.arange(L, dtype=f)
    angle = np.tile((t[:, None] * inv[None, :]).astype(f), (1, 2))
    base = ((half + f(0.4 * DH)) / f(1.4 * DH)).astype(f)
    power = ((t - L // 2) / f(WIN // 2)).astype(f)
    grow = np.tile((base[None, :] ** power[:, None]).astype(f), (1, 2))
    sign = np.repeat(np.array([-1, 1], f), DH // 2)
    for n, table in enumerate((np.cos(angle) * grow, np.sin(angle) * grow * sign,
                               np.cos(angle) * (f(1) / grow), np.sin(angle) * (f(1) / grow) * sign)):
        c[f"table{n}"] = np.ascontiguousarray(np.tile(table.astype(f).T, (2, 1)))
    return c


def lay_out(i):
    A = np.ascontiguousarray
    col = lambda v: A(v[:, None])

    def swapped(w, width):
        n = w.shape[-1]
        return A(w[..., np.arange(n).reshape(-1, 2, width // 2)[:, ::-1].reshape(-1)])

    def head_rows(w):
        o = np.zeros((P, GROUPS, C), w.dtype)
        for g in range(GROUPS):
            for h in range(HG):
                o[h * QUAD:h * QUAD + HD, g] = w[(g * HG + h) * HD:(g * HG + h + 1) * HD]
        return o

    d = {"x": A(i["L0_attn_batch"].reshape(T, C).T)}
    for n in "qkvo":
        d["ta_" + n] = A(i["L0_attn_W" + n].T)
        d["ta_b" + n] = i["L0_attn_b" + n][None, :] if n == "v" else col(i["L0_attn_b" + n])
    w = i["L0_ffn_attn_w"]
    d["cq"], d["ck"], d["cv"] = A(w[:, :C]), A(w[:, C:2 * C]), A(w[:, 2 * C:])
    d["cqs"], d["cks"] = swapped(d["cq"], HD), swapped(d["ck"], HD)
    d["cproj"] = head_rows(i["L0_ffn_proj_w"])
    d["taps"] = A(i["L0_ffn_conv_w"][:, 0, :])
    for n in (1, 2):
        d[f"ln{n}"] = A(np.stack([i[f"L0_ffn_ln{n}_w"], i[f"L0_ffn_ln{n}_b"]], 1))
    d["router"] = i["L0_ffn_router_w"]
    d["wv"] = A(i["L0_ffn_expert_wv"].transpose(1, 0, 2))
    d["wp"] = A(i["L0_ffn_expert_proj"].reshape(E, DFF // P, P, C).transpose(2, 0, 1, 3))
    w = i["L1_attn_w_qkv"].T
    d["dq"], d["dk"], d["dv"] = A(w[:, :C]), A(w[:, C:2 * C]), A(w[:, 2 * C:])
    d["dproj"] = head_rows(i["L1_attn_w_proj"].T)
    w = i["L1_ffn_Wqkv"]
    q, key, v = w[..., :INNER], w[..., INNER:2 * INNER], w[..., 2 * INNER:]
    pair = lambda m: m.reshape(LAYERS, C, PAIRS, P).transpose(0, 2, 1, 3)
    parts = [pair(q), pair(swapped(q, DH)), pair(key), pair(swapped(key, DH)), pair(v),
             i["L1_ffn_Wo"].reshape(LAYERS, PAIRS, P, C)]
    w = np.stack(parts, 3).reshape(LAYERS * PAIRS, P, 6, P)
    d["pair_w"] = A(np.concatenate([w, w[:1]]))
    cols = []
    for n in ("q", "k"):
        m = i[f"L1_ffn_{n}_scale"]
        for v in (m, np.concatenate([m[:, DH // 2:], m[:, :DH // 2]], 1)):
            cols.append(np.concatenate([v, v], 1))
    d["scales"] = A(np.stack(cols, 2))
    d["w1"] = i["L1_ffn_W1"]
    d["b1"], d["w2"] = np.zeros((LAYERS, P, 2 * NCHUNKS), np.float32), np.zeros((LAYERS, P, NCHUNKS, C), np.float32)
    for n, (o, m) in enumerate(DCH):
        d["b1"][:, :m, n] = i["L1_ffn_b1"][:, o:o + m]
        d["b1"][:, :m, NCHUNKS + n] = i["L1_ffn_b1"][:, DI + o:DI + o + m]
        d["w2"][:, :m, n] = i["L1_ffn_W2"][:, o:o + m]
    d["small"] = A(np.stack([i["L1_ffn_ln_g"], i["L1_ffn_ln_b"], i["L1_ffn_b2"]], 2))
    return d


def kernel(**inputs):
    import concourse.bacc as bacc
    from concourse.bass_utils import run_bass_kernel_spmd

    nc = bacc.Bacc("TRN2", target_bir_lowering=False, num_devices=1)
    host = {n: np.asarray(v) for n, v in inputs.items()}
    arrays, a = {}, {}
    for name, v in {**constants(), **lay_out(host)}.items():
        arrays["in_" + name] = np.ascontiguousarray(v)
        a[name] = nc.dram_tensor("in_" + name, v.shape, mybir.dt.from_np(v.dtype), kind="ExternalInput").ap()
    out = nc.dram_tensor("out", [C, T], F32, kind="ExternalOutput").ap()
    build_program(nc, a, out)
    result = run_bass_kernel_spmd(nc, [arrays], core_ids=[0])
    return np.ascontiguousarray(result.results[0]["out"].T).reshape(B, L, C)
```
